# Optimizing a Trainium2 kernel written in Bass

```python
import numpy as np
import jax
import jax.numpy as jnp

def _softmax(x, axis=-1):
    return jax.nn.softmax(x, axis=axis)
def _gelu(x):
    return jax.nn.gelu(x, approximate=True)
def _silu(x):
    return jax.nn.silu(x)
def _sigmoid(x):
    return jax.nn.sigmoid(x)
def _layernorm(x, axis=-1, eps=1e-5):
    m = jnp.mean(x, axis=axis, keepdims=True)
    v = jnp.var(x, axis=axis, keepdims=True)
    return (x - m) / jnp.sqrt(v + eps)
def _scatter_add(tgt, idx, src, axis=0):
    return tgt.at[idx].add(src)
def _segment_sum(src, seg, n):
    return jax.ops.segment_sum(src, seg, n)

kernel_name = 'mk_adj_preln_d2_adj_512_79061d'

def setup_inputs(seed: int = 0):
    np.random.seed(seed)
    _w = jnp.asarray
    def _rec_inputs():
        import jax
        import jax.numpy as jnp
        _gk = jax.random.key(seed)
        x = -0.0005207 + 1.001 * jax.random.normal(jax.random.fold_in(_gk, 1), (4096, 512), jnp.float32)
        _a = jax.random.bernoulli(jax.random.fold_in(_gk, 2), 0.00195312, (4096, 4096))
        _a = jnp.logical_or(_a, jnp.swapaxes(_a, -1, -2))
        _a = jnp.logical_or(_a, jnp.eye(4096, dtype=bool))
        _af = _a.astype(jnp.float32)
        adj = _af
        return x, adj
    x, adj = _rec_inputs()
    def _L0_gnn_setup():
        import jax, jax.numpy as jnp
        import numpy as np
        N = 4096
        IN = 512
        H = 8
        D = 64
        EDGE_PROB = 0.01
        key = jax.random.key(seed)
        kx, ka, kw, ko, kd = jax.random.split(key, 5)
        x = jax.random.normal(kx, (N, IN), dtype=jnp.float32)
        adj = (jax.random.uniform(ka, (N, N)) < EDGE_PROB).astype(jnp.float32)
        adj = jnp.maximum(adj, jnp.eye(N, dtype=jnp.float32))
        W = jax.random.normal(kw, (H, IN, D), dtype=jnp.float32) * (1.0 / np.sqrt(IN))
        a_origin = jax.random.normal(ko, (H, D), dtype=jnp.float32) * 0.1
        a_dst = jax.random.normal(kd, (H, D), dtype=jnp.float32) * 0.1
        return {'x': x, 'adj': adj, 'W': W, 'a_origin': a_origin, 'a_dst': a_dst}
    _L0_gnn_all = _L0_gnn_setup()
    _L0_gnn_in = {k: v for k, v in _L0_gnn_all.items() if k in ('W', 'a_origin', 'a_dst', )}
    del _L0_gnn_all

    def _L1_gnn_setup():
        import jax, jax.numpy as jnp
        import numpy as np
        N = 4096
        INPUT_DIM = 512
        KEY_DIM = 64
        OUT_DIM = 512
        N_HEADS = 8
        IDENTITY_BIAS = 0.01
        MASK_VAL = 1e+16

        def _xavier(key, shape, gain=np.sqrt(2.0)):
            std = gain * np.sqrt(2.0 / (shape[-2] + shape[-1]))
            return jax.random.normal(key, shape, dtype=jnp.float32) * np.float32(std)
        key = jax.random.key(seed)
        kx, ka, kk, kq, kv, ko = jax.random.split(key, 6)
        node_matrix = jax.random.normal(kx, (N, INPUT_DIM), dtype=jnp.float32)
        adjacency_matrix = jax.random.bernoulli(ka, 0.01, (N, N)).astype(jnp.float32)
        Wks = _xavier(kk, (N_HEADS, INPUT_DIM, KEY_DIM))
        Wqs = _xavier(kq, (N_HEADS, INPUT_DIM, KEY_DIM))
        Wvs = _xavier(kv, (N_HEADS, INPUT_DIM, KEY_DIM))
        Wo = _xavier(ko, (N_HEADS, KEY_DIM, OUT_DIM))
        return {'node_matrix': node_matrix, 'adjacency_matrix': adjacency_matrix, 'Wks': Wks, 'Wqs': Wqs, 'Wvs': Wvs, 'Wo': Wo}
    _L1_gnn_all = _L1_gnn_setup()
    _L1_gnn_in = {k: v for k, v in _L1_gnn_all.items() if k in ('Wks', 'Wqs', 'Wvs', 'Wo', )}
    del _L1_gnn_all

    return {
        "x": x,
        "adj": adj,
        "L0_gnn_W": _L0_gnn_in["W"],
        "L0_gnn_a_origin": _L0_gnn_in["a_origin"],
        "L0_gnn_a_dst": _L0_gnn_in["a_dst"],
        "L1_gnn_Wks": _L1_gnn_in["Wks"],
        "L1_gnn_Wqs": _L1_gnn_in["Wqs"],
        "L1_gnn_Wvs": _L1_gnn_in["Wvs"],
        "L1_gnn_Wo": _L1_gnn_in["Wo"],
    }

def reference(x, adj, L0_gnn_W, L0_gnn_a_origin, L0_gnn_a_dst, L1_gnn_Wks, L1_gnn_Wqs, L1_gnn_Wvs, L1_gnn_Wo):
    import jax
    import jax.numpy as jnp
    def _L0_gnn_ref(x, adj, W, a_origin, a_dst):
        import jax, jax.numpy as jnp
        import numpy as np
        N = 4096
        IN = 512
        H = 8
        D = 64
        EDGE_PROB = 0.01
        mx = jnp.einsum('nf,hfd->hnd', x, W)
        s_i = jnp.einsum('hnd,hd->hn', mx, a_origin)
        t_j = jnp.einsum('hnd,hd->hn', mx, a_dst)
        logits = s_i[:, :, None] + t_j[:, None, :]
        neg_inf = jnp.finfo(logits.dtype).min
        masked = jnp.where(adj[None] > 0, logits, neg_inf)
        attn = jax.nn.softmax(masked, axis=-1)
        out_h = jnp.einsum('hij,hjd->hid', attn, mx)
        return jnp.transpose(out_h, (1, 0, 2)).reshape(N, H * D)

    def _L1_gnn_ref(node_matrix, adjacency_matrix, Wks, Wqs, Wvs, Wo):
        import jax, jax.numpy as jnp
        import numpy as np
        N = 4096
        INPUT_DIM = 512
        KEY_DIM = 64
        OUT_DIM = 512
        N_HEADS = 8
        IDENTITY_BIAS = 0.01
        MASK_VAL = 1e+16

        def _xavier(key, shape, gain=np.sqrt(2.0)):
            std = gain * np.sqrt(2.0 / (shape[-2] + shape[-1]))
            return jax.random.normal(key, shape, dtype=jnp.float32) * np.float32(std)
        n = node_matrix.shape[0]
        kd = Wks.shape[-1]
        eye = jnp.eye(n, dtype=node_matrix.dtype)
        adj = jnp.maximum(adjacency_matrix, eye)
        q = jnp.einsum('nd,hdk->hnk', node_matrix, Wqs)
        k = jnp.einsum('nd,hdk->hnk', node_matrix, Wks)
        v = jnp.einsum('nd,hdk->hnk', node_matrix, Wvs)
        scores = jnp.einsum('hqk,hmk->hqm', q, k) * kd ** (-0.5)
        scores = scores + IDENTITY_BIAS * eye - MASK_VAL * (1.0 - adj)
        att = jax.nn.softmax(scores, axis=-1)
        return jnp.einsum('hqm,hmk,hko->qo', att, v, Wo)

    h = jnp.maximum(_layernorm(x, axis=-1), 0.0)
    x = x + _L0_gnn_ref(h, adj, L0_gnn_W, L0_gnn_a_origin, L0_gnn_a_dst)
    h = jnp.maximum(_layernorm(x, axis=-1), 0.0)
    x = x + _L1_gnn_ref(h, adj, L1_gnn_Wks, L1_gnn_Wqs, L1_gnn_Wvs, L1_gnn_Wo)
    return x


_drawn_inputs = setup_inputs


def setup_inputs(seed=0):
    import zlib

    import numpy as np

    out = dict(_drawn_inputs(seed))
    spreads = {}
    factors = {}
    for name, (base, spread) in spreads.items():
        noise = np.random.default_rng([zlib.crc32(name.encode()), seed]).standard_normal(out[name].shape)
        drawn = base * np.exp(spread * noise) if base else spread * noise
        out[name] = jnp.asarray(drawn.astype(out[name].dtype))
    for name, factor in factors.items():
        out[name] = (out[name] * factor).astype(out[name].dtype)
    return out
```

```python
from contextlib import ExitStack

import numpy as np

import concourse.bass as bass
from concourse import mybir

P = 128
F32 = mybir.dt.float32
F16 = mybir.dt.float16
I32 = mybir.dt.int32
BF16 = mybir.dt.bfloat16
ALU = mybir.AluOpType
ACT = mybir.ActivationFunctionType
AX_X = mybir.AxisListType.X
RMAX = bass.bass_isa.ReduceOp.max
ds = bass.ds

EPS = 1e-5
W_SCALE = 256.0
SHIFT_LEAST = -24.0
SHIFT_ROOM = 8.0 * float(np.log(4.0))
MASKED = -60000.0


def mask_constants(bias):
    a = (1.0 + np.arange(1024) / 1024.0).astype(np.float64)
    b = (bias / a).astype(np.float16).astype(np.float64)
    k = int(np.argmin(np.abs(a * b - bias)))
    return float(a[k]), float(b[k])


class Shapes:

    def __init__(self, x, w0):
        self.N, self.D = x.shape
        self.H, _, self.dh = w0.shape
        self.NT = self.N // P
        self.DC = self.D // P
        self.HG = self.H // 2
        self.GC = self.HG * self.dh + self.HG
        self.VC = 2 * self.dh + 1
        self.QB = 1024
        self.NB = self.N // self.QB
        self.QS = self.QB // P
        assert self.D == self.H * self.dh and self.D == 512 and self.dh == 64 and self.NT % 4 == 0


def in_pairs(eng, n, body):
    if n > 1:
        with eng.Fori(0, n - 1) as i:
            body(i, False)
    body(n - 1, True)


class Chain:

    def __init__(self, eng, sem, base=0):
        self.eng, self.sem, self.base, self.n = eng, sem, base, 0

    def __call__(self, ins):
        self.n += 1
        ins.then_inc(self.sem, 1)
        self.eng.wait_ge(self.sem, self.base + self.n)


class Scope:

    def __init__(self, nc, ctx, tag):
        self.nc, self.ctx, self.tag, self.sems = nc, ctx, tag, []

    def sb(self, name, shape, dt):
        return self.ctx.enter_context(self.nc.sbuf_tensor(f"{self.tag}_{name}", shape, dt))

    def ps(self, name, shape, dt=F32):
        return self.ctx.enter_context(self.nc.psum_tensor(f"{self.tag}_{name}", shape, dt))

    def sem(self, name):
        self.sems.append(self.nc.alloc_semaphore(name=f"{self.tag}_{name}"))
        return self.sems[-1]

    def block(self):
        self.ctx.callback(self.give_back)
        return self.ctx.enter_context(self.nc.Block())

    def give_back(self):
        self.nc.clear_and_free_semaphores(self.sems)
        self.nc.all_engine_barrier()


def make_constants(nc, c, mask_scale, diag_value):
    with ExitStack() as ctx:
        s = Scope(nc, ctx, "const")
        filled = s.sem("filled")
        block = s.block()

        @block.gpsimd
        def _(pool):
            tiles = [(c.ident, 1.0, 0.0), (c.ident_bf, 1.0, 0.0), (c.mask_ident, mask_scale, 0.0), (c.diag_mask, diag_value, MASKED)]
            for t, on, off in tiles:
                nc.gpsimd.memset(t[:], on).then_inc(filled, 1)
            pool.wait_ge(filled, len(tiles))
            for t, on, off in tiles:
                nc.gpsimd.affine_select(out=t[:], in_=t[:], compare_op=ALU.is_equal, fill=off, base=0,
                                        pattern=[[-1, P]], channel_multiplier=1)


def split_matmuls(nc, out, chunks):
    n = len(chunks)
    for j, (a, b) in enumerate(chunks):
        for k, (p, q) in enumerate(((0, 0), (0, 1), (1, 0))):
            mm = nc.tensor.matmul(out, a[:, p], b[:, q], start=j == 0 and k == 0, stop=j == n - 1 and k == 2)
    return mm


def raise_flag(nc, dve, link, good, bad, flag, spread_ready, spread):
    link(nc.vector.tensor_reduce(bad[:, 0:1], good, op=ALU.min, axis=AX_X))
    nc.vector.tensor_scalar(bad[:, 1:2], bad[:, 0:1], -1.0, 1.0, ALU.mult, ALU.add).then_inc(spread_ready, 1)
    dve.wait_ge(spread, 1)
    link(nc.vector.tensor_copy(flag[:], bad[0:1, 2:3]))


def spread_bad(nc, pool, bad, spread_ready, spread):
    pool.wait_ge(spread_ready, 1)
    nc.gpsimd.partition_all_reduce(bad[:, 2:3], bad[:, 1:2], P, RMAX).then_inc(spread, 1)


def gat_values(nc, sh, x, w0, a_dst, emx, parts, c):
    NT, DC, H, dh, HG, D = sh.NT, sh.DC, sh.H, sh.dh, sh.HG, sh.D
    CT = 4
    NC = NT // CT
    V = HG * dh
    lift = float(np.log(256.0)) if parts == 2 else 0.0
    with ExitStack() as ctx:
        s = Scope(nc, ctx, f"gv{parts}")
        w = s.sb("w", [P, DC, D], F32)
        w16 = s.sb("w16", [P, 2, DC, D], F16)
        adst = s.sb("adst", [P, D], F32)
        xm = s.sb("xm", [P, NT, D], F32)
        stats = s.sb("stats", [P, 2, CT, 6], F32)
        pair = s.sb("pair", [P, 2, CT, 2], F32)
        mv = s.sb("mv", [P, NT, 2], F32)
        rstd = s.sb("rstd", [P, NT], F32)
        shift = s.sb("shift", [P, NT], F32)
        h = s.sb("h", [P, 2, D], F32)
        hT = s.sb("hT", [P, 2, 2, D], F16)
        prod = s.sb("prod", [P, 2, D], F32)
        t_all = s.sb("t_all", [P, NT, H], F32)
        tmax = s.sb("tmax", [P, H], F32)
        tmax_all = s.sb("tmax_all", [P, H], F32)
        e_all = s.sb("e_all", [P, NT, H], F32)
        em = s.sb("em", [P, 2, 2, D], F32)
        consts = s.sb("consts", [P, 2], F32)
        psT = s.ps("psT", [P, 2, 512])
        psM = s.ps("psM", [P, 2, 512])

        w_in = s.sem("w_in")
        adst_in = s.sem("adst_in")
        x_in = [s.sem(f"x_in{k}") for k in range(2)]
        consts_set = s.sem("consts_set")
        stats_done = s.sem("stats_done")
        pair_done = s.sem("pair_done")
        mv_done = s.sem("mv_done")
        w_ready = s.sem("w_ready")
        waited = s.sem("waited")
        std_done = s.sem("std_done")
        norm_ready = s.sem("norm_ready")
        h_ready = s.sem("h_ready")
        turned = s.sem("turned")
        hi_ready = s.sem("hi_ready")
        lo_ready = s.sem("lo_ready")
        projected = s.sem("projected")
        mx_copied = s.sem("mx_copied")
        prod_done = s.sem("prod_done")
        t_done = s.sem("t_done")
        tmax_ready = s.sem("tmax_ready")
        tmax_spread = s.sem("tmax_spread")
        te_ready = s.sem("te_ready")
        e_ready = s.sem("e_ready")
        chain = s.sem("chain")
        em_ready = s.sem("em_ready")
        part_done = s.sem("part_done")
        rest_done = s.sem("rest_done")
        block = s.block()
        RS = parts - 1

        def emx_cols(n, q):
            return emx[:, ds(2 * n, 2), q, :].rearrange("p t (g v) -> p t g v", g=2)[:, :, :, 0:V]

        def flat(a):
            return a.rearrange("p t (g v) -> p t g v", g=2)

        @block.sync
        def _(sp):
            def load(i, k):
                sp.dma_start(xm[:, ds((2 * i + k) * CT, CT), :],
                             x[ds((2 * i + k) * (CT * P), CT * P), :].rearrange("(t p) d -> p t d", p=P)).then_inc(x_in[k], 16)

            load(0, 0)
            load(0, 1)
            if NC > 2:
                with sp.Fori(1, NC // 2) as i:
                    for k in range(2):
                        sp.wait_ge(x_in[k], 16 * i)
                        load(i, k)

        @block.gpsimd
        def _(pool):
            for k in range(DC):
                pool.dma_start(w[:, k, :].rearrange("p (h d) -> p h d", h=H),
                               w0[:, k * P:(k + 1) * P, :].rearrange("h p d -> p h d")).then_inc(w_in, 16)
            pool.dma_start(adst[:], a_dst.rearrange("(o h) d -> o (h d)", o=1).broadcast_to([P, D])).then_inc(adst_in, 16)
            pool.wait_ge(tmax_ready, 1)
            nc.gpsimd.partition_all_reduce(tmax_all[:], tmax[:], P, RMAX).then_inc(tmax_spread, 1)

        @block.scalar
        def _(act):
            act.sem_inc(mx_copied, 2)
            act.wait_ge(consts_set, 2)
            act.wait_ge(mv_done, NC + 2)
            nc.scalar.activation(rstd[:], mv[:, :, 1], ACT.Sqrt, bias=consts[:, 0:1]).then_inc(std_done, 1)
            act.wait_ge(norm_ready, 1)

            def relu_norm(t, k):
                act.wait_ge(turned, t + 1)
                nc.scalar.activation(h[:, k, :], xm[:, ds(t, 1), :], ACT.Relu, bias=shift[:, ds(t, 1)],
                                     scale=rstd[:, ds(t, 1)]).then_inc(h_ready, 1)

            def high(t, k):
                act.wait_ge(turned, t + 3)
                act.wait_ge(projected, t + 1)
                nc.scalar.activation(hT[:, k, 0, :], psT[:, k, :], ACT.Copy).then_inc(hi_ready, 1)

            def step(i, last):
                for k in range(2):
                    t = 2 * i + k
                    if not (last and k == 1):
                        high(t + 1, 1 - k)
                    if not last:
                        relu_norm(t + 2, k)
                    act.wait_ge(projected, t + 3)
                    nc.scalar.activation(xm[:, ds(t, 1), :], psM[:, k:k + 1, :], ACT.Copy, scale=1.0 / W_SCALE).then_inc(mx_copied, 1)

            relu_norm(0, 0)
            relu_norm(1, 1)
            high(0, 0)
            in_pairs(act, NT // 2, step)
            act.wait_ge(te_ready, 1)
            nc.scalar.activation(e_all[:], t_all[:], ACT.Exp, bias=consts[:, 1:2]).then_inc(e_ready, 1)

            with act.Fori(0, NT // 4) as i:
                for k in range(2):
                    n = 2 * i + k
                    act.wait_ge(em_ready, n + 1)
                    for q in range(RS):
                        if q > 0:
                            act.wait_ge(rest_done, RS * n + q + 2 * RS)
                        nc.scalar.activation(emx_cols(n, q), flat(em[:, k]), ACT.Copy).then_inc(part_done, 1)

        @block.tensor
        def _(pe):
            pe.sem_inc(turned, 2)
            pe.sem_inc(projected, 2)

            def turn(t, k):
                pe.wait_ge(h_ready, t + 1)
                pe.wait_ge(lo_ready, t + 1)
                for j in range(DC):
                    last = nc.tensor.transpose(psT[:, k, j * P:(j + 1) * P], h[:, k, j * P:(j + 1) * P], c.ident[:])
                last.then_inc(turned, 1)

            def step(i, last):
                for k in range(2):
                    t = 2 * i + k
                    if not (last and k == 1):
                        turn(t + 1, 1 - k)
                    pe.wait_ge(lo_ready, t + 3)
                    pe.wait_ge(mx_copied, t + 1)
                    mm = split_matmuls(nc, psM[:, k, :], [(hT[:, k, :, j * P:(j + 1) * P], w16[:, :, j, :]) for j in range(DC)])
                    mm.then_inc(projected, 1)

            turn(0, 0)
            pe.wait_ge(w_ready, 1)
            in_pairs(pe, NT // 2, step)

        @block.vector
        def _(dve):
            dve.sem_inc(pair_done, 2)
            dve.sem_inc(mv_done, 2)
            dve.sem_inc(lo_ready, 2)
            dve.sem_inc(t_done, 2)
            dve.sem_inc(rest_done, 2 * RS)
            nc.vector.memset(consts[:, 0:1], EPS).then_inc(consts_set, 1)
            nc.vector.memset(consts[:, 1:2], lift).then_inc(consts_set, 1)
            with dve.Fori(0, NC // 2) as i:
                for k in range(2):
                    n = 2 * i + k
                    dve.wait_ge(x_in[k], 16 * i + 16)
                    dve.wait_ge(pair_done, n + 1)
                    for m in range(CT):
                        st = nc.vector.bn_stats(stats[:, k, m, :], xm[:, ds(n * CT + m, 1), :])
                    st.then_inc(stats_done, 1)
                    dve.wait_ge(mv_done, n + 1)
                    dve.wait_ge(stats_done, n + 1)
                    dve.sem_inc(waited, 1)
                    for m in range(CT):
                        ag = nc.vector.bn_aggr(pair[:, k, m, :], stats[:, k, m, :])
                    ag.then_inc(pair_done, 1)
                    dve.wait_ge(pair_done, n + 3)
                    nc.vector.tensor_copy(mv[:, ds(n * CT, CT), :], pair[:, k]).then_inc(mv_done, 1)
            dve.wait_ge(std_done, 1)
            link = Chain(dve, chain)
            link(nc.vector.reciprocal(rstd[:], rstd[:]))
            nc.vector.scalar_tensor_tensor(shift[:], mv[:, :, 0], -1.0, rstd[:], ALU.mult, ALU.mult).then_inc(norm_ready, 1)
            dve.wait_ge(w_in, 16 * DC)
            link(nc.vector.tensor_scalar(w16[:, 0], w[:], W_SCALE, None, ALU.mult))
            nc.vector.scalar_tensor_tensor(w16[:, 1], w[:], W_SCALE, w16[:, 0], ALU.mult, ALU.subtract).then_inc(w_ready, 1)
            dve.wait_ge(adst_in, 16)

            def low(t, k):
                dve.wait_ge(hi_ready, t + 1)
                nc.vector.tensor_tensor(hT[:, k, 1, :], psT[:, k, :], hT[:, k, 0, :], ALU.subtract).then_inc(lo_ready, 1)

            def step(i, last):
                for k in range(2):
                    t = 2 * i + k
                    if not (last and k == 1):
                        low(t + 1, 1 - k)
                    dve.wait_ge(mx_copied, t + 3)
                    dve.wait_ge(t_done, t + 1)
                    nc.vector.tensor_tensor(prod[:, k, :], xm[:, ds(t, 1), :].rearrange("p o n -> p (o n)"), adst[:], ALU.mult).then_inc(prod_done, 1)
                    dve.wait_ge(prod_done, t + 1)
                    nc.vector.tensor_reduce(t_all[:, ds(t, 1), :], prod[:, k, :].rearrange("p (h d) -> p h d", h=H),
                                            op=ALU.add, axis=AX_X).then_inc(t_done, 1)

            low(0, 0)
            in_pairs(dve, NT // 2, step)
            dve.wait_ge(t_done, NT + 2)
            nc.vector.tensor_reduce(tmax[:], t_all[:].rearrange("p t h -> p h t"), op=ALU.max, axis=AX_X).then_inc(tmax_ready, 1)
            dve.wait_ge(tmax_spread, 1)
            nc.vector.tensor_tensor(t_all[:], t_all[:], tmax_all[:].unsqueeze(1).broadcast_to([P, NT, H]), ALU.subtract).then_inc(te_ready, 1)
            dve.wait_ge(e_ready, 1)

            def weigh(n, k):
                dve.wait_ge(rest_done, RS * n + RS)
                nc.vector.tensor_tensor(em[:, k].rearrange("p t (h d) -> p (t h) d", h=H),
                                        xm[:, ds(2 * n, 2), :].rearrange("p t (h d) -> p (t h) d", h=H),
                                        e_all[:, ds(2 * n, 2), :].rearrange("p t h -> p (t h)").unsqueeze(2).broadcast_to([P, 2 * H, dh]),
                                        ALU.mult).then_inc(em_ready, 1)

            def rests(n, k):
                for q in range(RS):
                    dve.wait_ge(part_done, RS * n + q + 1)
                    to = flat(em[:, k]) if q < RS - 1 else emx_cols(n, RS)
                    nc.vector.tensor_tensor(to, flat(em[:, k]), emx_cols(n, q), ALU.subtract).then_inc(rest_done, 1)

            def split_step(i, last):
                for k in range(2):
                    n = 2 * i + k
                    if not (last and k == 1):
                        weigh(n + 1, 1 - k)
                    rests(n, k)

            weigh(0, 0)
            in_pairs(dve, NT // 4, split_step)
            for g in range(2):
                of = e_all[:, :, g * HG:(g + 1) * HG]
                for q in range(parts):
                    to = emx[:, :, q, g * sh.GC + V:(g + 1) * sh.GC]
                    link(nc.vector.tensor_copy(to, of))
                    if q < parts - 1:
                        link(nc.vector.tensor_tensor(of, of, to, ALU.subtract))


def gat_attention(nc, sh, x, adj, emx, parts, mv1, maskD, x1D, flag, c):
    NT, H, dh, HG, N = sh.NT, sh.H, sh.dh, sh.HG, sh.N
    TG = 8
    NG = NT // TG if NT >= TG else 1
    TG = NT // NG
    with ExitStack() as ctx:
        s = Scope(nc, ctx, f"ga{parts}")
        rows = s.sb("rows", [P, 2, N], F32)
        rows01 = s.sb("rows01", [P, 2, N], BF16)
        colsT = s.sb("colsT", [P, 2, N], BF16)
        mask = s.sb("mask", [P, 2, N], F16)
        xt = s.sb("xt", [P, 2, sh.D], F32)
        x1 = s.sb("x1", [P, 2, sh.D], F32)
        rsum = s.sb("rsum", [P, NT, 2, HG], F32)
        good = s.sb("good", [P, NT * (H + 1)], F32)
        bad = s.sb("bad", [P, 3], F32)
        stats = s.sb("stats", [P, 2, 6], F32)
        pair = s.sb("pair", [P, 2, 2], F32)
        psT = s.ps("psT", [P, 4, 1024], BF16)
        psO = s.ps("psO", [P, 2, 2, 512])

        rows_in = [s.sem(f"rows_in{k}") for k in range(2)]
        x_in = [s.sem(f"x_in{k}") for k in range(2)]
        cast = s.sem("cast")
        turned = s.sem("turned")
        cols_ready = s.sem("cols_ready")
        summed = s.sem("summed")
        masked = s.sem("masked")
        x1_ready = s.sem("x1_ready")
        mask_out = [s.sem(f"mask_out{k}") for k in range(2)]
        x1_out = [s.sem(f"x1_out{k}") for k in range(2)]
        stats_done = s.sem("stats_done")
        chain = s.sem("chain")
        raised = s.sem("raised")
        bad_ready = s.sem("bad_ready")
        bad_spread = s.sem("bad_spread")
        waited = s.sem("waited")
        block = s.block()

        @block.sync
        def _(sp):
            for k in range(2):
                sp.dma_start(rows[:, k, :], adj[k * P:(k + 1) * P, :]).then_inc(rows_in[k], 16)
            for k in range(2):
                sp.sem_inc(mask_out[k], 16)
                sp.sem_inc(x1_out[k], 16)

            def step(i, last):
                for k in range(2):
                    t = 2 * i + k
                    sp.wait_ge(x1_ready, t + 1)
                    sp.dma_start(xt[:, k, :], x[ds(t * P, P), :]).then_inc(x_in[k], 16)
                    if not last:
                        sp.wait_ge(cast, t + 1)
                        sp.dma_start(rows[:, k, :], adj[ds((t + 2) * P, P), :]).then_inc(rows_in[k], 16)
                    sp.wait_ge(masked, t + 3)
                    sp.dma_start(maskD[ds(t, 1)].rearrange("o p n -> (o p) n"), mask[:, k, :]).then_inc(mask_out[k], 16)
                    sp.wait_ge(x1_ready, t + 3)
                    sp.dma_start(x1D[ds(t * P, P), :], x1[:, k, :]).then_inc(x1_out[k], 16)

            in_pairs(sp, NT // 2, step)
            for k in range(2):
                sp.wait_ge(mask_out[k], 16 * (NT // 2) + 16)
                sp.wait_ge(x1_out[k], 16 * (NT // 2) + 16)

        @block.tensor
        def _(pe):
            pe.sem_inc(turned, 2 * NG)
            pe.sem_inc(summed, 2)

            def turn(t, k):
                pe.wait_ge(cast, t + 1)
                for g in range(NG):
                    pe.wait_ge(cols_ready, NG * t + g + 1)
                    for j in range(TG):
                        col = (g * TG + j) * P
                        last = nc.tensor.transpose(psT[:, g, j * P:(j + 1) * P], rows01[:, k, col:col + P], c.ident_bf[:])
                    last.then_inc(turned, 1)

            def step(i, last):
                for k in range(2):
                    t = 2 * i + k
                    if not (last and k == 1):
                        turn(t + 1, 1 - k)
                    pe.wait_ge(cols_ready, NG * t + 2 * NG)
                    pe.wait_ge(x1_ready, t + 1)
                    for j in range(NT):
                        for g in range(2):
                            for q in range(parts):
                                mm = nc.tensor.matmul(psO[:, k, g, 0:sh.GC], colsT[:, k, j * P:(j + 1) * P],
                                                      emx[:, j, q, g * sh.GC:(g + 1) * sh.GC],
                                                      start=j == 0 and q == 0, stop=j == NT - 1 and q == parts - 1)
                    mm.then_inc(summed, 1)

            turn(0, 0)
            in_pairs(pe, NT // 2, step)

        @block.scalar
        def _(act):
            act.sem_inc(cols_ready, NG)

            def step(i, last):
                for k in range(2):
                    t = 2 * i + k
                    act.wait_ge(summed, t + 1)
                    act.wait_ge(masked, t + 1)
                    for g in range(NG):
                        act.wait_ge(turned, NG * t + 2 * NG + g + 1)
                        nc.scalar.activation(colsT[:, k, g * TG * P:(g + 1) * TG * P], psT[:, g, 0:TG * P], ACT.Copy).then_inc(cols_ready, 1)

            in_pairs(act, NT // 2, step)

        @block.vector
        def _(dve):
            dve.sem_inc(masked, 2)
            dve.sem_inc(x1_ready, 2)
            dve.sem_inc(stats_done, 2)

            def cast_rows(t, k):
                dve.wait_ge(rows_in[k], (t - k) * 8 + 16)
                dve.wait_ge(turned, NG * t + NG)
                nc.vector.tensor_scalar(rows01[:, k, :], rows[:, k, :], 0.0, None, ALU.is_gt).then_inc(cast, 1)

            def make_mask(t, k):
                dve.wait_ge(cols_ready, NG * t + 2 * NG)
                dve.wait_ge(mask_out[k], (t - k) * 8 + 16)
                nc.vector.tensor_scalar(mask[:, k, :], colsT[:, k, :], -MASKED, MASKED, ALU.mult, ALU.add).then_inc(raised, 1)
                dve.wait_ge(raised, t + 1)
                diag = mask[:, k, ds(t * P, P)]
                nc.vector.tensor_tensor(diag, diag, c.diag_mask[:], ALU.max).then_inc(masked, 1)

            STEPS = 4

            def finish(t, k):
                link = Chain(dve, chain, STEPS * t)
                dve.wait_ge(summed, t + 3)
                sums = psO[:, k, :, HG * dh:sh.GC]
                rs = rsum[:, ds(t, 1)].rearrange("p o g h -> p (o g) h")
                link(nc.vector.reciprocal(rs, sums))
                dve.wait_ge(x1_out[k], (t - k) * 8 + 16)
                link(nc.vector.tensor_tensor(x1[:, k, :].rearrange("p (g h d) -> p g h d", g=2, h=HG),
                                             psO[:, k, :, 0:HG * dh].rearrange("p g (h d) -> p g h d", h=HG),
                                             rs.unsqueeze(3).broadcast_to([P, 2, HG, dh]), ALU.mult))
                dve.wait_ge(x_in[k], (t - k) * 8 + 16)
                nc.vector.tensor_tensor(x1[:, k, :], x1[:, k, :], xt[:, k, :], ALU.add).then_inc(x1_ready, 1)
                dve.wait_ge(x1_ready, t + 3)
                link(nc.vector.bn_stats(stats[:, k, :], x1[:, k, :]))
                dve.sem_inc(waited, 1)
                link(nc.vector.bn_aggr(pair[:, k, :], stats[:, k, :]))
                nc.vector.tensor_copy(mv1[:, ds(t, 1), :], pair[:, k:k + 1, :]).then_inc(stats_done, 1)
                assert link.n == STEPS

            def step(i, last):
                for k in range(2):
                    t = 2 * i + k
                    if not last:
                        cast_rows(t + 2, k)
                    if not (last and k == 1):
                        make_mask(t + 1, 1 - k)
                    finish(t, k)

            cast_rows(0, 0)
            cast_rows(1, 1)
            make_mask(0, 0)
            in_pairs(dve, NT // 2, step)
            if flag is not None:
                dve.wait_ge(stats_done, NT + 2)
                link = Chain(dve, chain, STEPS * NT)
                link(nc.vector.tensor_scalar(good[:, 0:NT * H], rsum[:].rearrange("p t g h -> p (t g h)"), 1.0, None, ALU.is_le))
                link(nc.vector.tensor_scalar(good[:, NT * H:], mv1[:, :, 1], 1e30, None, ALU.is_lt))
                raise_flag(nc, dve, link, good[:], bad, flag, bad_ready, bad_spread)

        if flag is not None:
            @block.gpsimd
            def _(pool):
                spread_bad(nc, pool, bad, bad_ready, bad_spread)


def qkv(nc, sh, x1D, wq, wk, wv, mv1, d, c):
    NT, DC, H, dh, D, VC = sh.NT, sh.DC, sh.H, sh.dh, sh.D, sh.VC
    GT = 4
    NGR = NT // GT
    OUTS = 2 * DC + GT
    with ExitStack() as ctx:
        s = Scope(nc, ctx, "qkv")
        w = s.sb("w", [P, 3, DC, D], F32)
        w16 = s.sb("w16", [P, 3, 2, DC, D], F16)
        xt = s.sb("xt", [P, 2, GT, D], F32)
        h = s.sb("h", [P, 2, GT, D], F32)
        hT = s.sb("hT", [P, 2, DC, 2, GT * P], F16)
        hi = s.sb("hi", [P, 2, 2 * DC, 512], F16)
        lo = s.sb("lo", [P, 2, 2 * DC, 512], F16)
        v = s.sb("v", [P, 2, H, GT, VC], F16)
        own = s.sb("own", [P, DC, 512], BF16)
        heads = s.sb("heads", [P, DC, H], BF16)
        shift16 = s.sb("shift16", [H, 2, 512], F16)
        rstd = s.sb("rstd", [P, NT], F32)
        shift = s.sb("shift", [P, NT], F32)
        eps = s.sb("eps", [P, 1], F32)
        psT = s.ps("psT", [P, 2, 512])
        psP = s.ps("psP", [P, 4, 512])
        psD = s.ps("psD", [P, 512])

        w_in = [s.sem(f"w_in{n}") for n in range(3)]
        x_in = [s.sem(f"x_in{k}") for k in range(2)]
        eps_set = s.sem("eps_set")
        heads_clear = s.sem("heads_clear")
        heads_set = s.sem("heads_set")
        std_done = s.sem("std_done")
        chain = s.sem("chain")
        w_ready = s.sem("w_ready")
        norm_ready = s.sem("norm_ready")
        ones_set = s.sem("ones_set")
        h_ready = s.sem("h_ready")
        turned = s.sem("turned")
        hT_hi = s.sem("hT_hi")
        hT_ready = s.sem("hT_ready")
        projected = s.sem("projected")
        waited = s.sem("waited")
        hi_ready = s.sem("hi_ready")
        lo_ready = s.sem("lo_ready")
        own_ready = s.sem("own_ready")
        own_summed = s.sem("own_summed")
        shift_ready = s.sem("shift_ready")
        parts_out = [s.sem(f"parts_out{k}") for k in range(2)]
        OUT_INC = 16 * (4 * DC + H + 1)
        block = s.block()

        @block.gpsimd
        def _(pool):
            for n, m in enumerate((wq, wk, wv)):
                for k in range(DC):
                    pool.dma_start(w[:, n, k, :].rearrange("p (h d) -> p h d", h=H),
                                   m[:, k * P:(k + 1) * P, :].rearrange("h p d -> p h d")).then_inc(w_in[n], 16)
            with pool.Fori(0, NGR // 2) as i:
                for k in range(2):
                    t = 2 * i + k
                    pool.wait_ge(h_ready, t + 1)
                    pool.dma_start(xt[:, k], x1D[ds(t * (GT * P), GT * P), :].rearrange("(t p) d -> p t d", p=P)).then_inc(x_in[k], 16)

        @block.sync
        def _(sp):
            for k in range(2):
                sp.sem_inc(parts_out[k], OUT_INC)

            with sp.Fori(0, NGR // 2) as i:
                for k in range(2):
                    t = 2 * i + k
                    tok = ds(t * (GT * P), GT * P)
                    for n in range(2 * DC):
                        hiD, loD = (d.qhi, d.qlo) if n < DC else (d.khi, d.klo)
                        r = (n % DC) * P
                        sp.wait_ge(lo_ready, OUTS * t + n + 5)
                        if n == 0:
                            sp.sem_inc(waited, 1)
                        sp.dma_start(hiD[r:r + P, tok], hi[:, k, n, :]).then_inc(parts_out[k], 16)
                        sp.dma_start(loD[r:r + P, tok], lo[:, k, n, :]).then_inc(parts_out[k], 16)
                    sp.wait_ge(shift_ready, t + 2)
                    sp.dma_start(d.shift[:, tok], shift16[:, k, :]).then_inc(parts_out[k], 16)
                    sp.wait_ge(lo_ready, OUTS * t + OUTS + 4)
                    sp.sem_inc(waited, 1)
                    for hh in range(H):
                        sp.dma_start(d.v[hh, :, ds(t * GT * VC, GT * VC)], v[:, k, hh].rearrange("p t c -> p (t c)")).then_inc(parts_out[k], 16)
            for k in range(2):
                sp.wait_ge(parts_out[k], OUT_INC * (NGR // 2 + 1))

        @block.tensor
        def _(pe):
            pe.sem_inc(turned, 2 * DC)
            pe.sem_inc(projected, 2 * OUTS)
            pe.sem_inc(own_summed, 1)

            def turn(t, k):
                pe.wait_ge(h_ready, t + 3)
                for j in range(DC):
                    pe.wait_ge(hT_ready, DC * t + j + 1)
                    for g in range(GT):
                        tr = nc.tensor.transpose(psT[:, j % 2, g * P:(g + 1) * P], h[:, k, g, j * P:(j + 1) * P], c.ident[:])
                    tr.then_inc(turned, 1)

            def step(i, last):
                for k in range(2):
                    t = 2 * i + k
                    if not (last and k == 1):
                        turn(t + 1, 1 - k)
                    pe.wait_ge(hT_ready, DC * t + DC + 2)
                    for n in range(OUTS):
                        pe.wait_ge(lo_ready, OUTS * t + n + 1)
                        if n < 2 * DC:
                            r = (n % DC) * P
                            chunks = [(w16[:, n // DC, :, j, r:r + P], hT[:, k, j]) for j in range(DC)]
                        else:
                            g = n - 2 * DC
                            chunks = [(hT[:, k, j, :, g * P:(g + 1) * P], w16[:, 2, :, j, :]) for j in range(DC)]
                        split_matmuls(nc, psP[:, n % 4, :], chunks).then_inc(projected, 1)
                    pe.wait_ge(own_ready, DC * t + DC)
                    pe.wait_ge(shift_ready, t + 1)
                    for n in range(DC):
                        mm = nc.tensor.matmul(psD[0:H, :], heads[:, n, :], own[:, n, :], start=n == 0, stop=n == DC - 1)
                    mm.then_inc(own_summed, 1)

            turn(0, 0)
            pe.wait_ge(w_ready, 3)
            pe.wait_ge(heads_set, H)
            in_pairs(pe, NGR // 2, step)

        @block.scalar
        def _(act):
            act.sem_inc(h_ready, 2)
            act.wait_ge(eps_set, 1)
            nc.scalar.activation(rstd[:], mv1[:, :, 1], ACT.Sqrt, bias=eps[:]).then_inc(std_done, 1)
            act.wait_ge(norm_ready, 1)

            def relu_norm(t, k):
                act.wait_ge(x_in[k], (t - k) * 8 + 16)
                act.wait_ge(turned, DC * t + DC)
                for g in range(GT):
                    r = nc.scalar.activation(h[:, k, g, :], xt[:, k, g, :], ACT.Relu, bias=shift[:, ds(t * GT + g, 1)],
                                             scale=rstd[:, ds(t * GT + g, 1)])
                r.then_inc(h_ready, 1)

            def high(t, k):
                act.wait_ge(projected, OUTS * t + OUTS)
                for j in range(DC):
                    act.wait_ge(turned, DC * t + 2 * DC + j + 1)
                    nc.scalar.activation(hT[:, k, j, 0, :], psT[:, j % 2, :], ACT.Copy).then_inc(hT_hi, 1)

            def step(i, last):
                for k in range(2):
                    t = 2 * i + k
                    if not (last and k == 1):
                        high(t + 1, 1 - k)
                    if not last:
                        relu_norm(t + 2, k)
                    act.wait_ge(parts_out[k], (t - k) * (OUT_INC // 2) + OUT_INC)
                    for n in range(OUTS):
                        act.wait_ge(projected, OUTS * t + 2 * OUTS + n + 1)
                        if n < 2 * DC:
                            to, of = hi[:, k, n, :], psP[:, n % 4, :]
                        else:
                            to = v[:, k, :, n - 2 * DC, 0:dh]
                            of = psP[:, n % 4, :].rearrange("p (h d) -> p h d", h=H)
                        nc.scalar.activation(to, of, ACT.Copy, scale=1.0 / W_SCALE).then_inc(hi_ready, 1)

            relu_norm(0, 0)
            relu_norm(1, 1)
            high(0, 0)
            in_pairs(act, NGR // 2, step)

        @block.vector
        def _(dve):
            dve.sem_inc(hT_ready, 2)
            dve.sem_inc(lo_ready, 4)
            dve.sem_inc(shift_ready, 1)
            nc.vector.memset(eps[:], EPS).then_inc(eps_set, 1)
            nc.vector.memset(heads[:], 0.0).then_inc(heads_clear, 1)
            nc.vector.memset(v[:, :, :, :, dh:dh + 1], 1.0).then_inc(ones_set, 1)
            dve.wait_ge(heads_clear, 1)
            for hh in range(H):
                r = (hh % 2) * dh
                nc.vector.memset(heads[r:r + dh, hh // 2, hh:hh + 1], -1.0).then_inc(heads_set, 1)
            dve.wait_ge(std_done, 1)
            link = Chain(dve, chain)
            link(nc.vector.reciprocal(rstd[:], rstd[:]))
            nc.vector.scalar_tensor_tensor(shift[:], mv1[:, :, 0], -1.0, rstd[:], ALU.mult, ALU.mult).then_inc(norm_ready, 1)
            dve.wait_ge(ones_set, 1)
            def low_T(t, k):
                for j in range(DC):
                    dve.wait_ge(hT_hi, DC * t + j + 1)
                    nc.vector.tensor_tensor(hT[:, k, j, 1, :], psT[:, j % 2, :], hT[:, k, j, 0, :], ALU.subtract).then_inc(hT_ready, 1)

            def step(i, last):
                for k in range(2):
                    t = 2 * i + k
                    if not (last and k == 1):
                        low_T(t + 1, 1 - k)
                    for n in range(OUTS):
                        dve.wait_ge(hi_ready, OUTS * t + n + 1)
                        if n < 2 * DC:
                            to, of, high = lo[:, k, n, :], psP[:, n % 4, :], hi[:, k, n, :]
                        else:
                            g = n - 2 * DC
                            to, high = v[:, k, :, g, dh + 1:VC], v[:, k, :, g, 0:dh]
                            of = psP[:, n % 4, :].rearrange("p (h d) -> p h d", h=H)
                        nc.vector.scalar_tensor_tensor(to, of, 1.0 / W_SCALE, high, ALU.mult, ALU.subtract).then_inc(lo_ready, 1)
                        if DC <= n < 2 * DC:
                            if n == DC:
                                dve.wait_ge(own_summed, t + 1)
                            nc.vector.tensor_tensor(own[:, n - DC, :], hi[:, k, n - DC, :], hi[:, k, n, :], ALU.mult).then_inc(own_ready, 1)
                    dve.wait_ge(own_summed, t + 2)
                    nc.vector.tensor_scalar(shift16[:, k, :], psD[0:H, :], -SHIFT_LEAST, -SHIFT_ROOM, ALU.min, ALU.add).then_inc(shift_ready, 1)

            for n in range(3):
                dve.wait_ge(w_in[n], 16 * DC)
                link(nc.vector.tensor_scalar(w16[:, n, 0], w[:, n], W_SCALE, None, ALU.mult))
                nc.vector.scalar_tensor_tensor(w16[:, n, 1], w[:, n], W_SCALE, w16[:, n, 0], ALU.mult, ALU.subtract).then_inc(w_ready, 1)
            low_T(0, 0)
            in_pairs(dve, NGR // 2, step)


def row_maxima(nc, sh, adj, d, c):
    NT, H, dh, N = sh.NT, sh.H, sh.dh, sh.N
    KC = min(2048, N)
    NK = N // KC
    with ExitStack() as ctx:
        s = Scope(nc, ctx, "mx")
        ks = s.sb("ks", [P, H, N], F16)
        qt = s.sb("qt", [P, 2, H, P], F16)
        rows = s.sb("rows", [P, 2, N], F32)
        mask = s.sb("mask", [P, 2, N], F16)
        junk = s.sb("junk", [P, 2, KC], F16)
        part = s.sb("part", [P, 2, H, NK], F32)
        top = s.sb("top", [P, H, NT], F32)
        topT = s.sb("topT", [P, 2, P], F16)
        ps = s.ps("ps", [P, 2, KC])

        keys_in = s.sem("keys_in")
        q_in = [s.sem(f"q_in{k}") for k in range(2)]
        rows_in = [s.sem(f"rows_in{k}") for k in range(2)]
        mask_ready = s.sem("mask_ready")
        scored = s.sem("scored")
        reduced = s.sem("reduced")
        tile_done = s.sem("tile_done")
        waited = s.sem("waited")
        turned = s.sem("turned")
        top_ready = s.sem("top_ready")
        top_out = s.sem("top_out")
        block = s.block()
        COLS = H * NT
        NCB = -(-COLS // P)
        CB = COLS // NCB

        @block.gpsimd
        def _(pool):
            for h in range(H):
                pool.dma_start(ks[0:dh, h, :], d.khi[h * dh:(h + 1) * dh, :]).then_inc(keys_in, 16)
                pool.dma_start(ks[dh:P, h, :], d.klo[h * dh:(h + 1) * dh, :]).then_inc(keys_in, 16)

        @block.sync
        def _(sp):
            with sp.Fori(0, NT // 2) as i:
                for k in range(2):
                    t = 2 * i + k
                    sp.wait_ge(mask_ready, t + 1)
                    sp.dma_start(rows[:, k, :], adj[ds(t * P, P), :]).then_inc(rows_in[k], 16)
                    sp.wait_ge(scored, (t + 1) * (H * NK))
                    sp.sem_inc(waited, 1)
                    src = d.qhi[:, ds(t * P, P)].rearrange("(h d) n -> d h n", h=H)
                    sp.dma_start(qt[0:dh, k], src).then_inc(q_in[k], 16)
                    sp.dma_start(qt[dh:P, k], src).then_inc(q_in[k], 16)
            for b in range(NCB):
                sp.wait_ge(top_ready, b + 1)
                sp.dma_start(d.shift.rearrange("h (t p) -> (h t) p", p=P)[b * CB:(b + 1) * CB, :], topT[0:CB, b, :]).then_inc(top_out, 16)
            sp.wait_ge(top_out, 16 * NCB)

        @block.scalar
        def _(act):
            act.sem_inc(mask_ready, 2)
            with act.Fori(0, NT // 2) as i:
                for k in range(2):
                    t = 2 * i + k
                    act.wait_ge(rows_in[k], 16 * i + 16)
                    act.wait_ge(tile_done, t + 1)
                    nc.scalar.activation(mask[:, k, :], rows[:, k, :], ACT.Copy, scale=-MASKED, bias=MASKED).then_inc(mask_ready, 1)

        @block.tensor
        def _(pe):
            pe.sem_inc(scored, 2 * H * NK)
            pe.wait_ge(keys_in, 16 * 2 * H)
            with pe.Fori(0, NT // 2) as i:
                for k in range(2):
                    t = 2 * i + k
                    pe.wait_ge(q_in[k], 32 * i + 32)
                    for h in range(H):
                        for m in range(NK):
                            n = h * NK + m
                            pe.wait_ge(reduced, t * (H * NK) + n + 1)
                            for j in range(KC // 512):
                                col = m * KC + j * 512
                                mm = nc.tensor.matmul(ps[:, n % 2, j * 512:(j + 1) * 512], qt[:, k, h, :],
                                                      ks[:, h, col:col + 512], start=True, stop=True)
                            mm.then_inc(scored, 1)
            pe.wait_ge(tile_done, NT + 2)
            for b in range(NCB):
                nc.tensor.transpose(ps[0:CB, b, 0:P], top[:].rearrange("p h t -> p (h t)")[:, b * CB:(b + 1) * CB], c.ident[:]).then_inc(turned, 1)

        @block.vector
        def _(dve):
            dve.sem_inc(reduced, 2)
            dve.sem_inc(tile_done, 2)
            with dve.Fori(0, NT // 2) as i:
                for k in range(2):
                    t = 2 * i + k
                    dve.wait_ge(mask_ready, t + 3)
                    for n in range(H * NK):
                        dve.wait_ge(scored, (t + 2) * (H * NK) + n + 1)
                        dve.wait_ge(reduced, t * (H * NK) + n + 1)
                        dve.sem_inc(waited, 1)
                        m = n % NK
                        nc.vector.tensor_tensor_reduce(out=junk[:, n % 2, :], in0=ps[:, n % 2, :], in1=mask[:, k, m * KC:(m + 1) * KC],
                                                       scale=1.0, scalar=-3e38, op0=ALU.add, op1=ALU.max,
                                                       accum_out=part[:, k, n // NK, m:m + 1]).then_inc(reduced, 1)
                    dve.wait_ge(reduced, (t + 1) * (H * NK) + 2)
                    nc.vector.tensor_reduce(top[:, :, ds(t, 1)].rearrange("p h o -> p (h o)"), part[:, k], op=ALU.max, axis=AX_X).then_inc(tile_done, 1)
            for b in range(NCB):
                dve.wait_ge(turned, b + 1)
                nc.vector.tensor_scalar(topT[0:CB, b, :], ps[0:CB, b, 0:P], -1.0, None, ALU.mult).then_inc(top_ready, 1)


def attention(nc, sh, maskD, d, c, scale, tag, flag):
    NT, H, dh, N, VC, QB, QS = sh.NT, sh.H, sh.dh, sh.N, sh.VC, sh.QB, sh.QS
    HALF = QB // 512
    NI = sh.NB * H
    OB = 3
    NOB = -(-QS // OB)
    KV_INC = 16 * 8
    NP = NT // 2
    MC = 4
    MP = NP // MC
    with ExitStack() as ctx:
        s = Scope(nc, ctx, tag)
        mask = s.sb("mask", [P, QS, NT * P], F16)
        ks = s.sb("ks", [P, 2, N], F16)
        kb = s.sb("kb", [dh + 1, 2, N], F16)
        v = s.sb("v", [P, 2, NT * VC], F16)
        qa = s.sb("qa", [P, 2, QB], F16)
        qb = s.sb("qb", [dh + 1, 2, QB], F16)
        e = s.sb("e", [P, 2, QB], F32)
        phi = s.sb("phi", [P, 2, QB], F16)
        plo = s.sb("plo", [P, 2, QB], F16)
        o = s.sb("o", [P, 2, QS, VC], F32)
        onum = s.sb("onum", [P, QS, dh], F32)
        oinv = s.sb("oinv", [P, NI, QS], F32)
        good = s.sb("good", [P, 2, NI * QS], F32)
        bad = s.sb("bad", [P, 3], F32)
        att = s.sb("att", [P, 2, QS, dh], F32)
        psS = s.ps("psS", [P, 2, QB])
        psO = s.ps("psO", [P, NOB, 512])

        ones_set = s.sem("ones_set")
        mask_in = [s.sem(f"mask_in{m}") for m in range(MC)]
        item_in = [s.sem(f"item_in{k}") for k in range(2)]
        scored = s.sem("scored")
        exp_done = s.sem("exp_done")
        hi_done = s.sem("hi_done")
        lo_done = s.sem("lo_done")
        applied = s.sem("applied")
        bad_ready = s.sem("bad_ready")
        bad_spread = s.sem("bad_spread")
        o_copied = s.sem("o_copied")
        o_read = s.sem("o_read")
        att_ready = s.sem("att_ready")
        att_out = [s.sem(f"att_out{k}") for k in range(2)]
        chain = s.sem("chain")
        waited = s.sem("waited")
        block = s.block()

        @block.sync
        def _(sp):
            for k in range(2):
                sp.sem_inc(att_out[k], 16)

            def load(it, k):
                b, h = it // H, it % H
                qcols, hrows = ds(b * QB, QB), ds(h * dh, dh)
                for to, of in ((ks[0:dh, k, :], d.khi[hrows, :]), (ks[dh:P, k, :], d.klo[hrows, :]), (kb[0:dh, k, :], d.khi[hrows, :]),
                               (v[:, k, :], d.v[ds(h, 1)].rearrange("o p c -> (o p) c")),
                               (qa[0:dh, k, :], d.qhi[hrows, qcols]), (qa[dh:P, k, :], d.qhi[hrows, qcols]),
                               (qb[0:dh, k, :], d.qlo[hrows, qcols]), (qb[dh:dh + 1, k, :], d.shift[ds(h, 1), qcols])):
                    sp.dma_start(to, of).then_inc(item_in[k], 16)

            def step(i, last):
                for k in range(2):
                    it = 2 * i + k
                    b, h = it // H, it % H
                    sp.wait_ge(att_ready, it + 1)
                    sp.dma_start(d.att[ds(b * QB, QB), ds(h * dh, dh)].rearrange("(q p) d -> p q d", p=P), att[:, k]).then_inc(att_out[k], 16)
                    if not last:
                        load(it + 2, k)

            load(0, 0)
            load(1, 1)
            in_pairs(sp, NI // 2, step)
            for k in range(2):
                sp.wait_ge(att_out[k], 16 * (NI // 2) + 16)

        @block.gpsimd
        def _(pool):
            def load_mask(b, m):
                cols = slice(m * 2 * MP * P, (m + 1) * 2 * MP * P)
                pool.dma_start(mask[:, :, cols], maskD[ds(b * QS, QS), :, cols].rearrange("q p n -> p q n")).then_inc(mask_in[m], 16)

            for m in range(MC):
                load_mask(0, m)
            if sh.NB > 1:
                with pool.Fori(1, sh.NB) as b:
                    for m in range(MC):
                        pool.wait_ge(scored, (b * H - 1) * NT + (m + 1) * 2 * MP)
                        load_mask(b, m)
            if flag is not None:
                spread_bad(nc, pool, bad, bad_ready, bad_spread)

        @block.tensor
        def _(pe):
            pe.sem_inc(applied, 2)
            pe.wait_ge(ones_set, 1)

            def score(it, kt, par, k, first):
                g = it * NT + kt
                if not first:
                    pe.wait_ge(exp_done, g - 1)
                cols = ds(kt * P, P)
                for f in range(HALF):
                    q = slice(f * 512, (f + 1) * 512)
                    out = psS[:, par, q]
                    nc.tensor.matmul(out, ks[:, k, cols], qa[:, k, q], start=True, stop=False)
                    nc.tensor.matmul(out, kb[:, k, cols], qb[:, k, q], start=False, stop=False)
                    mm = nc.tensor.matmul(out.rearrange("p (q n) -> p q n", n=P), c.mask_ident[:], mask[:, f * 4:(f + 1) * 4, cols], start=False, stop=True)
                mm.then_inc(scored, 1)

            def apply(it, kt, par, k, first=False):
                g = it * NT + kt
                pe.wait_ge(lo_done, g + 3)
                for q in range(QS):
                    o_cols = psO[:, q // OB, (q % OB) * VC:(q % OB + 1) * VC]
                    qc = slice(q * P, (q + 1) * P)
                    nc.tensor.matmul(o_cols, phi[:, par, qc], v[:, k, ds(kt * VC, VC)], start=first and q % OB == 0, stop=False, skip_group_check=True)
                    mm = nc.tensor.matmul(o_cols[:, 0:dh + 1], plo[:, par, qc], v[:, k, ds(kt * VC, dh + 1)], start=False, stop=False, skip_group_check=True)
                return mm

            def begin(it, k):
                pe.wait_ge(item_in[k], (it - k) * (KV_INC // 2) + KV_INC)
                pe.wait_ge(mask_in[0], (it // H) * 16 + 16)

            def step(i, last):
                for k in range(2):
                    it = 2 * i + k
                    for m in range(MC):
                        if m > 0:
                            pe.wait_ge(mask_in[m], (it // H) * 16 + 16)
                            pe.sem_inc(waited, 1)
                        first, end = max(1, m * MP), (m + 1) * MP
                        if first == 1 and end > 1:
                            score(it, 2, 0, k, False)
                            if k == 1 or not isinstance(i, int) or i > 0:
                                pe.wait_ge(o_copied, it + 1)
                            apply(it, 0, 0, k, True).then_inc(applied, 1)
                            score(it, 3, 1, k, False)
                            apply(it, 1, 1, k).then_inc(applied, 1)
                            first = 2
                        if first < end:
                            with pe.Fori(first, end) as j:
                                for n in range(2):
                                    score(it, 2 * j + n, n, k, False)
                                    apply(it, 2 * j + n - 2, n, k).then_inc(applied, 1)
                    more = not (last and k == 1)
                    if more:
                        begin(it + 1, 1 - k)
                        score(it + 1, 0, 0, 1 - k, False)
                    apply(it, NT - 2, 0, k).then_inc(applied, 1)
                    if more:
                        score(it + 1, 1, 1, 1 - k, False)
                    apply(it, NT - 1, 1, k).then_inc(applied, 1)

            begin(0, 0)
            score(0, 0, 0, 0, True)
            score(0, 1, 1, 0, True)
            in_pairs(pe, NI // 2, step)

        @block.scalar
        def _(act):
            act.sem_inc(o_copied, 1)

            def weigh(it, kt, par):
                g = it * NT + kt
                act.wait_ge(scored, g + 1)
                act.wait_ge(lo_done, g + 1)
                nc.scalar.activation(e[:, par, :], psS[:, par, :], ACT.Exp, scale=scale).then_inc(exp_done, 1)

            def step(i, last):
                for k in range(2):
                    it = 2 * i + k
                    with act.Fori(1, NT // 2) as j:
                        for m in range(2):
                            weigh(it, 2 * j + m, m)
                    if not (last and k == 1):
                        weigh(it + 1, 0, 0)
                        weigh(it + 1, 1, 1)
                    act.wait_ge(applied, (it + 1) * NT + 2)
                    act.wait_ge(o_read, it + 1)
                    for b in range(NOB):
                        q0, q1 = b * OB, min(QS, b * OB + OB)
                        cp = nc.scalar.activation(o[:, k, q0:q1, :], psO[:, b, 0:(q1 - q0) * VC].rearrange("p (q c) -> p q c", c=VC), ACT.Copy)
                    cp.then_inc(o_copied, 1)

            weigh(0, 0, 0)
            weigh(0, 1, 1)
            in_pairs(act, NI // 2, step)

        @block.vector
        def _(dve):
            dve.sem_inc(lo_done, 2)
            dve.sem_inc(o_read, 2)
            nc.vector.memset(kb[dh:dh + 1, :, :], 1.0).then_inc(ones_set, 1)

            def split(it, kt, par):
                g = it * NT + kt
                dve.wait_ge(exp_done, g + 1)
                dve.wait_ge(applied, g + 1)
                nc.vector.tensor_copy(phi[:, par, :], e[:, par, :]).then_inc(hi_done, 1)
                dve.wait_ge(hi_done, g + 1)
                nc.vector.tensor_tensor(plo[:, par, :], e[:, par, :], phi[:, par, :], ALU.subtract).then_inc(lo_done, 1)

            STEPS = 1

            def step(i, last):
                for k in range(2):
                    it = 2 * i + k
                    with dve.Fori(1, NT // 2) as j:
                        for m in range(2):
                            split(it, 2 * j + m, m)
                    if not (last and k == 1):
                        split(it + 1, 0, 0)
                        split(it + 1, 1, 1)
                    dve.wait_ge(o_copied, it + 2)
                    inv = oinv[:, ds(it, 1), :].rearrange("p o q -> p (o q)")
                    nc.vector.reciprocal(inv, o[:, k, :, dh]).then_inc(chain, 1)
                    nc.vector.tensor_tensor(onum[:], o[:, k, :, 0:dh], o[:, k, :, dh + 1:VC], ALU.add).then_inc(o_read, 1)
                    dve.wait_ge(chain, it + 1)
                    dve.wait_ge(o_read, it + 3)
                    dve.wait_ge(att_out[k], (it - k) * 8 + 16)
                    nc.vector.tensor_tensor(att[:, k], onum[:], inv.unsqueeze(2).broadcast_to([P, QS, dh]), ALU.mult).then_inc(att_ready, 1)
                    dve.wait_ge(att_ready, it + 1)
                    dve.sem_inc(waited, 1)

            split(0, 0, 0)
            split(0, 1, 1)
            in_pairs(dve, NI // 2, step)
            if flag is not None:
                link = Chain(dve, chain, NI)
                of = oinv[:].rearrange("p i q -> p (i q)")
                link(nc.vector.tensor_scalar(good[:, 0, :], of, 16.0, None, ALU.is_le))
                link(nc.vector.tensor_scalar(good[:, 1, :], of, 0.0, None, ALU.is_gt))
                raise_flag(nc, dve, link, good[:].rearrange("p a n -> p (a n)"), bad, flag, bad_ready, bad_spread)


def output_projection(nc, sh, wo, x1D, d, out, c):
    NT, DC, D = sh.NT, sh.DC, sh.D
    CT = 4
    NC = NT // CT
    with ExitStack() as ctx:
        s = Scope(nc, ctx, "op")
        w = s.sb("w", [P, DC, D], F32)
        w16 = s.sb("w16", [P, DC, 2, D], F16)
        at = s.sb("at", [P, NC, CT, D], F32)
        xt = s.sb("xt", [P, 2, CT, D], F32)
        atT = s.sb("atT", [P, 2, 2, D], F16)
        y = s.sb("y", [P, 2, CT, D], F32)
        psT = s.ps("psT", [P, 2, 512])
        psY = s.ps("psY", [P, 2, 512])

        w_in = s.sem("w_in")
        at_in = [s.sem(f"at_in{n}") for n in range(NC)]
        x_in = [s.sem(f"x_in{k}") for k in range(2)]
        hi_weights = s.sem("hi_weights")
        w_ready = s.sem("w_ready")
        turned = s.sem("turned")
        hi_ready = s.sem("hi_ready")
        atT_ready = s.sem("atT_ready")
        projected = s.sem("projected")
        y_ready = s.sem("y_ready")
        y_out = [s.sem(f"y_out{k}") for k in range(2)]
        block = s.block()

        @block.gpsimd
        def _(pool):
            pool.dma_start(w[:], wo.rearrange("h k o -> (h k) o").rearrange("(c p) o -> p c o", p=P)).then_inc(w_in, 16)

        @block.sync
        def _(sp):
            def load_x(n, k):
                sp.dma_start(xt[:, k], x1D[ds(n * (CT * P), CT * P), :].rearrange("(t p) d -> p t d", p=P)).then_inc(x_in[k], 16)

            for n in range(NC):
                sp.dma_start(at[:, n], d.att[n * CT * P:(n + 1) * CT * P, :].rearrange("(t p) d -> p t d", p=P)).then_inc(at_in[n], 16)
                if n < 2:
                    load_x(n, n)
                    sp.sem_inc(y_out[n], 16)
            for n in range(NC):
                k = n % 2
                sp.wait_ge(y_ready, CT * n + 3 * CT)
                sp.dma_start(out[n * CT * P:(n + 1) * CT * P, :].rearrange("(t p) d -> p t d", p=P), y[:, k]).then_inc(y_out[k], 16)
                if n + 2 < NC:
                    load_x(n + 2, k)
            for k in range(2):
                sp.wait_ge(y_out[k], 16 * (NC // 2) + 16)

        @block.scalar
        def _(act):
            for t in range(NT):
                k = t % 2
                act.wait_ge(turned, t + 1)
                act.wait_ge(projected, t + 1)
                nc.scalar.activation(atT[:, k, 0, :], psT[:, k, :], ACT.Copy).then_inc(hi_ready, 1)

        @block.tensor
        def _(pe):
            pe.sem_inc(projected, 2)

            def turn(t):
                k = t % 2
                pe.wait_ge(at_in[t // CT], 16)
                pe.wait_ge(atT_ready, t + 1)
                for j in range(DC):
                    tr = nc.tensor.transpose(psT[:, k, j * P:(j + 1) * P], at[:, t // CT, t % CT, j * P:(j + 1) * P], c.ident[:])
                tr.then_inc(turned, 1)

            turn(0)
            pe.wait_ge(w_ready, 1)
            for t in range(NT):
                k = t % 2
                if t + 1 < NT:
                    turn(t + 1)
                pe.wait_ge(atT_ready, t + 3)
                pe.wait_ge(y_ready, t + 2 * CT - 1)
                split_matmuls(nc, psY[:, k, :], [(atT[:, k, :, j * P:(j + 1) * P], w16[:, j]) for j in range(DC)]).then_inc(projected, 1)

        @block.vector
        def _(dve):
            dve.sem_inc(atT_ready, 2)
            dve.sem_inc(y_ready, 2 * CT)
            dve.wait_ge(w_in, 16)
            nc.vector.tensor_scalar(w16[:, :, 0, :], w[:], W_SCALE, None, ALU.mult).then_inc(hi_weights, 1)
            dve.wait_ge(hi_weights, 1)
            nc.vector.scalar_tensor_tensor(w16[:, :, 1, :], w[:], W_SCALE, w16[:, :, 0, :], ALU.mult, ALU.subtract).then_inc(w_ready, 1)

            def low(t):
                k = t % 2
                dve.wait_ge(hi_ready, t + 1)
                nc.vector.tensor_tensor(atT[:, k, 1, :], psT[:, k, :], atT[:, k, 0, :], ALU.subtract).then_inc(atT_ready, 1)

            low(0)
            for t in range(NT):
                n, m = t // CT, t % CT
                if t + 1 < NT:
                    low(t + 1)
                dve.wait_ge(projected, t + 3)
                if m == 0:
                    dve.wait_ge(x_in[n % 2], 16 * (n // 2) + 16)
                    dve.wait_ge(y_out[n % 2], 16 * (n // 2) + 16)
                nc.vector.scalar_tensor_tensor(y[:, n % 2, m, :], psY[:, t % 2, :], 1.0 / W_SCALE, xt[:, n % 2, m, :], ALU.mult, ALU.add).then_inc(y_ready, 1)


class Holder:
    pass


def two_graph_layers(nc, x, adj, w0, a_dst, wk, wq, wv, wo, out):
    sh = Shapes(x, w0)
    N, NT, H = sh.N, sh.NT, sh.H
    scale = float(sh.dh) ** -0.5
    mask_scale, diag_value = mask_constants(0.01 / scale)

    def dram(name, shape, dt):
        return nc.dram_tensor(name, shape, dt, kind="Internal").ap()

    maskD = dram("mask_tiles", (NT, P, N), F16)
    x1D = dram("x1", (N, sh.D), F32)
    d = Holder()
    d.qhi, d.qlo, d.khi, d.klo = (dram(n, (sh.D, N), F16) for n in ("q_high", "q_low", "k_high", "k_low"))
    d.v = dram("v_parts", (H, P, NT * sh.VC), F16)
    d.shift = dram("shift", (H, N), F16)
    d.att = dram("att", (N, sh.D), F32)

    with ExitStack() as ctx:
        s = Scope(nc, ctx, "all")
        c = Holder()
        c.ident = s.sb("ident", [P, P], F32)
        c.ident_bf = s.sb("ident_bf", [P, P], BF16)
        c.mask_ident = s.sb("mask_ident", [P, P], F16)
        c.diag_mask = s.sb("diag_mask", [P, P], F16)
        mv1 = s.sb("mv1", [P, NT, 2], F32)
        make_constants(nc, c, mask_scale, diag_value)
        flag0 = s.sb("flag0", [1, 1], I32)
        flag1 = s.sb("flag1", [1, 1], I32)

        def layer0(parts, dt, flag):
            with ExitStack() as ctx0:
                emx = Scope(nc, ctx0, f"l0_{parts}").sb("emx", [P, NT, parts, 2 * sh.GC], dt)
                gat_values(nc, sh, x, w0, a_dst, emx, parts, c)
                gat_attention(nc, sh, x, adj, emx, parts, mv1, maskD, x1D, flag, c)

        layer0(2, F16, flag0)
        with nc.If(nc.values_load(flag0[0:1, 0:1], min_val=0, max_val=1) > 0):
            layer0(3, BF16, None)
        qkv(nc, sh, x1D, wq, wk, wv, mv1, d, c)
        attention(nc, sh, maskD, d, c, scale, "at", flag1)
        with nc.If(nc.values_load(flag1[0:1, 0:1], min_val=0, max_val=1) > 0):
            row_maxima(nc, sh, adj, d, c)
            attention(nc, sh, maskD, d, c, scale, "at2", None)
        output_projection(nc, sh, wo, x1D, d, out, c)


_INS = ["x", "adj", "L0_gnn_W", "L0_gnn_a_dst", "L1_gnn_Wks", "L1_gnn_Wqs", "L1_gnn_Wvs", "L1_gnn_Wo"]


def kernel(**inputs):
    import numpy as _np
    import concourse.bacc as _bacc
    from concourse import mybir as _mybir
    from concourse.bass_utils import run_bass_kernel_spmd as _run

    nc = _bacc.Bacc("TRN2", target_bir_lowering=False, num_devices=1)
    arrays, args = {}, []
    for name in _INS:
        a = _np.ascontiguousarray(inputs[name])
        arrays[f"in_{name}"] = a
        args.append(nc.dram_tensor(f"in_{name}", a.shape, _mybir.dt.from_np(a.dtype), kind="ExternalInput").ap())
    out = nc.dram_tensor("out_x", inputs["x"].shape, _mybir.dt.float32, kind="ExternalOutput").ap()
    two_graph_layers(nc, *args, out)
    r = _run(nc, [arrays], core_ids=[0])
    return r.results[0]["out_x"]
```

```python
from contextlib import ExitStack

import numpy as np

import concourse.bass as bass
from concourse import mybir

P = 128
F32 = mybir.dt.float32
F16 = mybir.dt.float16
I32 = mybir.dt.int32
BF16 = mybir.dt.bfloat16
ALU = mybir.AluOpType
ACT = mybir.ActivationFunctionType
AX_X = mybir.AxisListType.X
RMAX = bass.bass_isa.ReduceOp.max
ds = bass.ds

EPS = 1e-5
E_MOST = 256.0
W_SCALE = 32.0
MASKED = -60000.0


def mask_constants(bias):
    a = (1.0 + np.arange(1024) / 1024.0).astype(np.float64)
    b = (bias / a).astype(np.float16).astype(np.float64)
    k = int(np.argmin(np.abs(a * b - bias)))
    return float(a[k]), float(b[k])


class Shapes:

    def __init__(self, x, w0):
        self.N, self.D = x.shape
        self.H, _, self.dh = w0.shape
        self.NT = self.N // P
        self.DC = self.D // P
        self.HG = self.H // 2
        self.GC = self.HG * self.dh + self.HG
        self.VC = 2 * self.dh + 1
        self.QB = 1024
        self.NB = self.N // self.QB
        self.QS = self.QB // P
        assert self.D == self.H * self.dh and self.D == 512 and self.dh == 64 and self.NT % 8 == 0


def in_pairs(eng, n, body):
    if n > 1:
        with eng.Fori(0, n - 1) as i:
            body(i, False)
    body(n - 1, True)


class Chain:

    def __init__(self, eng, sem, base=0):
        self.eng, self.sem, self.base, self.n = eng, sem, base, 0

    def __call__(self, ins):
        self.n += 1
        ins.then_inc(self.sem, 1)
        self.eng.wait_ge(self.sem, self.base + self.n)


class Scope:

    def __init__(self, nc, ctx, tag):
        self.nc, self.ctx, self.tag, self.sems = nc, ctx, tag, []

    def sb(self, name, shape, dt):
        return self.ctx.enter_context(self.nc.sbuf_tensor(f"{self.tag}_{name}", shape, dt))

    def ps(self, name, shape, dt=F32):
        return self.ctx.enter_context(self.nc.psum_tensor(f"{self.tag}_{name}", shape, dt))

    def sem(self, name):
        self.sems.append(self.nc.alloc_semaphore(name=f"{self.tag}_{name}"))
        return self.sems[-1]

    def block(self):
        self.ctx.callback(self.give_back)
        return self.ctx.enter_context(self.nc.Block())

    def give_back(self):
        self.nc.clear_and_free_semaphores(self.sems)
        self.nc.all_engine_barrier()


def make_constants(nc, c, mask_scale, diag_value):
    with ExitStack() as ctx:
        s = Scope(nc, ctx, "const")
        filled = s.sem("filled")
        block = s.block()

        @block.gpsimd
        def _(pool):
            tiles = [(c.ident, 1.0, 0.0), (c.ident_bf, 1.0, 0.0), (c.mask_ident, mask_scale * W_SCALE, 0.0), (c.diag_mask, diag_value, MASKED)]
            for t, on, off in tiles:
                nc.gpsimd.memset(t[:], on).then_inc(filled, 1)
            pool.wait_ge(filled, len(tiles))
            for t, on, off in tiles:
                nc.gpsimd.affine_select(out=t[:], in_=t[:], compare_op=ALU.is_equal, fill=off, base=0,
                                        pattern=[[-1, P]], channel_multiplier=1)


def split_matmuls(nc, out, chunks):
    n = len(chunks)
    for j, (a, b) in enumerate(chunks):
        for k, (p, q) in enumerate(((0, 0), (0, 1), (1, 0))):
            mm = nc.tensor.matmul(out, a[:, p], b[:, q], start=j == 0 and k == 0, stop=j == n - 1 and k == 2)
    return mm


def raise_flag(nc, dve, link, good, bad, flag, spread_ready, spread):
    link(nc.vector.tensor_reduce(bad[:, 0:1], good, op=ALU.min, axis=AX_X))
    nc.vector.tensor_scalar(bad[:, 1:2], bad[:, 0:1], -1.0, 1.0, ALU.mult, ALU.add).then_inc(spread_ready, 1)
    dve.wait_ge(spread, 1)
    link(nc.vector.tensor_copy(flag[:], bad[0:1, 2:3]))


def spread_bad(nc, pool, bad, spread_ready, spread):
    pool.wait_ge(spread_ready, 1)
    nc.gpsimd.partition_all_reduce(bad[:, 2:3], bad[:, 1:2], P, RMAX).then_inc(spread, 1)


def gat_values(nc, sh, x, w0, a_dst, xm, t_all, emx, c):
    NT, DC, H, dh, HG, D = sh.NT, sh.DC, sh.H, sh.dh, sh.HG, sh.D
    CT = 4
    NC = NT // CT
    V = HG * dh
    DH = D + H
    with ExitStack() as ctx:
        s = Scope(nc, ctx, "gv" if emx is not None else "gv_rows")
        w = s.sb("w", [P, DC, D], F32)
        w16 = s.sb("w16", [P, 2, DC, DH], F16)
        wprod = s.sb("wprod", [P, DC, D], F32)
        wt = s.sb("wt", [P, DC, H], F32)
        adst = s.sb("adst", [P, D], F32)
        stats = s.sb("stats", [P, NT, 6], F32)
        mv = s.sb("mv", [P, NT, 2], F32)
        rstd = s.sb("rstd", [P, NT], F32)
        shift = s.sb("shift", [P, NT], F32)
        h = s.sb("h", [P, 2, D], F32)
        hT = s.sb("hT", [P, 2, 2, D], F16)
        tmax = s.sb("tmax", [P, H], F32)
        tmax_all = s.sb("tmax_all", [P, H], F32)
        e_all = s.sb("e_all", [P, NT, H], F32)
        em = s.sb("em", [P, 2, D], F32)
        log_most = s.sb("log_most", [P, 1], F32)
        eps = s.sb("eps", [P, 1], F32)
        psT = s.ps("psT", [P, 2, 512])
        psM = s.ps("psM", [P, 2, 512])
        psE = s.ps("psE", [P, 2, 512])

        w_in = s.sem("w_in")
        adst_in = s.sem("adst_in")
        x_in = [s.sem(f"x_in{k}") for k in range(2)]
        consts_set = s.sem("consts_set")
        std_done = s.sem("std_done")
        stats_done = s.sem("stats_done")
        mv_done = s.sem("mv_done")
        w_hi = s.sem("w_hi")
        w_chain = s.sem("w_chain")
        w_ready = s.sem("w_ready")
        waited = s.sem("waited")
        norm_ready = s.sem("norm_ready")
        h_ready = s.sem("h_ready")
        turned = s.sem("turned")
        hi_ready = s.sem("hi_ready")
        lo_ready = s.sem("lo_ready")
        projected = s.sem("projected")
        mx_copied = s.sem("mx_copied")
        t_done = s.sem("t_done")
        tmax_ready = s.sem("tmax_ready")
        tmax_spread = s.sem("tmax_spread")
        te_ready = s.sem("te_ready")
        e_ready = s.sem("e_ready")
        chain = s.sem("chain")
        e_high = s.sem("e_high")
        em_ready = s.sem("em_ready")
        part_done = s.sem("part_done")
        rest_done = s.sem("rest_done")
        block = s.block()

        BATCHES = [range(0, CT), range(CT, 2 * CT)] + ([range(2 * CT, NT)] if NC > 2 else [])
        SPREAD = 6

        def tiles(b):
            return slice(BATCHES[b].start, BATCHES[b].stop)

        def emx_cols(t, q):
            return emx[:, ds(t, 1), q, :].rearrange("p t (g v) -> p (t g) v", g=2)[:, :, 0:V]

        def flat(a):
            return a.rearrange("p (g v) -> p g v", g=2)

        def chunk_pairs(eng, body):
            n = NC // 2
            body(0, True, n == 1)
            if n > 2:
                with eng.Fori(1, n - 1) as i:
                    body(i, False, False)
            if n > 1:
                body(n - 1, False, True)

        @block.sync
        def _(sp):
            def load(i, k):
                sp.dma_start(xm[:, ds((2 * i + k) * CT, CT), :],
                             x[ds((2 * i + k) * (CT * P), CT * P), :].rearrange("(t p) d -> p t d", p=P)).then_inc(x_in[k], 16)

            load(0, 0)
            load(0, 1)
            if NC > 2:
                with sp.Fori(1, NC // 2) as i:
                    for k in range(2):
                        sp.wait_ge(x_in[k], 16 * i)
                        load(i, k)

        @block.gpsimd
        def _(pool):
            for k in range(DC):
                pool.dma_start(w[:, k, :].rearrange("p (h d) -> p h d", h=H),
                               w0[:, k * P:(k + 1) * P, :].rearrange("h p d -> p h d")).then_inc(w_in, 16)
            pool.dma_start(adst[:], a_dst.rearrange("(o h) d -> o (h d)", o=1).broadcast_to([P, D])).then_inc(adst_in, 16)
            if emx is not None:
                pool.wait_ge(tmax_ready, 1)
                nc.gpsimd.partition_all_reduce(tmax_all[:], tmax[:], P, RMAX).then_inc(tmax_spread, 1)

        @block.scalar
        def _(act):
            act.sem_inc(mx_copied, 2)
            act.wait_ge(consts_set, 2)

            def std(b):
                act.wait_ge(mv_done, b + 1)
                nc.scalar.activation(rstd[:, tiles(b)], mv[:, tiles(b), 1], ACT.Sqrt, bias=eps[:]).then_inc(std_done, 1)

            def relu_norm(t, k):
                act.wait_ge(turned, t + 1)
                nc.scalar.activation(h[:, k, :], xm[:, ds(t, 1), :], ACT.Relu, bias=shift[:, ds(t, 1)],
                                     scale=rstd[:, ds(t, 1)]).then_inc(h_ready, 1)

            def high(t, k):
                act.wait_ge(turned, t + 3)
                act.wait_ge(projected, t + 1)
                nc.scalar.activation(hT[:, k, 0, :], psT[:, k, :], ACT.Copy).then_inc(hi_ready, 1)

            def exp(n):
                act.wait_ge(te_ready, n + 1)
                e = e_all[:, ds(n * CT, CT), :]
                nc.scalar.activation(e, e, ACT.Exp, bias=log_most[:]).then_inc(e_ready, 1)

            def part(t, k):
                act.wait_ge(em_ready, t + 1)
                nc.scalar.activation(emx_cols(t, 0), flat(em[:, k]), ACT.Copy).then_inc(part_done, 1)

            def step(i, first, last):
                for kc in range(2):
                    n = 2 * i + kc
                    more = not (last and kc == 1)
                    before = emx is not None and not (first and kc == 0)
                    for m in range(CT):
                        t, k = CT * n + m, m % 2
                        if more or m < CT - 1:
                            high(t + 1, 1 - k)
                        if more or m < CT - 2:
                            if m == CT - 2 and first:
                                act.wait_ge(norm_ready, n + 2)
                            relu_norm(t + 2, k)
                        if m == 0 and before:
                            exp(n - 1)
                        if before:
                            part(t - CT, k)
                        if first and not last and CT * kc + m == SPREAD - 1:
                            std(2)
                        act.wait_ge(projected, t + 3)
                        act.sem_inc(waited, 1)
                        nc.scalar.activation(xm[:, ds(t, 1), :], psM[:, k:k + 1, :], ACT.Copy, scale=1.0 / W_SCALE).then_inc(mx_copied, 1)

            std(0)
            act.wait_ge(w_in, 16 * DC)
            nc.scalar.activation(w16[:, 0, :, 0:D], w[:], ACT.Copy, scale=W_SCALE).then_inc(w_hi, 1)
            act.wait_ge(norm_ready, 1)
            relu_norm(0, 0)
            relu_norm(1, 1)
            high(0, 0)
            std(1)
            chunk_pairs(act, step)
            if emx is not None:
                exp(NC - 1)
                for m in range(CT):
                    part(NT - CT + m, m % 2)

        @block.tensor
        def _(pe):
            pe.sem_inc(turned, 2)
            pe.sem_inc(projected, 2)

            def turn(t, k):
                pe.wait_ge(h_ready, t + 1)
                pe.wait_ge(lo_ready, t + 1)
                for j in range(DC):
                    last = nc.tensor.transpose(psT[:, k, j * P:(j + 1) * P], h[:, k, j * P:(j + 1) * P], c.ident[:])
                last.then_inc(turned, 1)

            def step(i, last):
                for k in range(2):
                    t = 2 * i + k
                    if not (last and k == 1):
                        turn(t + 1, 1 - k)
                    pe.wait_ge(lo_ready, t + 3)
                    pe.wait_ge(mx_copied, t + 1)
                    split_matmuls(nc, psM[:, k, :], [(hT[:, k, :, j * P:(j + 1) * P], w16[:, :, j, 0:D]) for j in range(DC)])
                    pe.wait_ge(w_ready, 2)
                    pe.wait_ge(t_done, t + 1)
                    mm = split_matmuls(nc, psE[:, k, 0:H], [(hT[:, k, :, j * P:(j + 1) * P], w16[:, :, j, D:DH]) for j in range(DC)])
                    mm.then_inc(projected, 1)

            turn(0, 0)
            pe.wait_ge(w_ready, 1)
            in_pairs(pe, NT // 2, step)

        @block.vector
        def _(dve):
            dve.sem_inc(lo_ready, 2)
            dve.sem_inc(t_done, 2)
            dve.sem_inc(rest_done, 2)
            nc.vector.memset(log_most[:], float(np.log(E_MOST))).then_inc(consts_set, 1)
            nc.vector.memset(eps[:], EPS).then_inc(consts_set, 1)

            def statistics(of):
                for t in of:
                    dve.wait_ge(x_in[t // CT % 2], 16 * (t // CT // 2) + 16)
                    nc.vector.bn_stats(stats[:, t, :], xm[:, t, :]).then_inc(stats_done, 1)

            def moments(b):
                dve.wait_ge(stats_done, BATCHES[b].stop)
                for t in BATCHES[b]:
                    ag = nc.vector.bn_aggr(mv[:, t, :], stats[:, t, :])
                ag.then_inc(mv_done, 1)

            def norms(b):
                r = rstd[:, tiles(b)]
                dve.wait_ge(std_done, b + 1)
                nc.vector.reciprocal(r, r).then_inc(chain, 1)
                dve.wait_ge(chain, b + 1)
                nc.vector.scalar_tensor_tensor(shift[:, tiles(b)], mv[:, tiles(b), 0], -1.0, r, ALU.mult, ALU.mult).then_inc(norm_ready, 1)

            def low(t, k):
                dve.wait_ge(hi_ready, t + 1)
                nc.vector.tensor_tensor(hT[:, k, 1, :], psT[:, k, :], hT[:, k, 0, :], ALU.subtract).then_inc(lo_ready, 1)

            def t_less_shift(n):
                tc = ds(n * CT, CT)
                dve.wait_ge(t_done, CT * n + CT + 2)
                dve.wait_ge(tmax_spread, 1)
                nc.vector.tensor_tensor(e_all[:, tc, :], t_all[:, tc, :], tmax_all[:].unsqueeze(1).broadcast_to([P, CT, H]), ALU.subtract).then_inc(te_ready, 1)

            def weigh(t, k):
                dve.wait_ge(mx_copied, t + 3)
                dve.wait_ge(rest_done, t + 1)
                nc.vector.tensor_tensor(em[:, k].rearrange("p (h d) -> p h d", h=H),
                                        xm[:, ds(t, 1), :].rearrange("p t (h d) -> p (t h) d", h=H),
                                        e_all[:, ds(t, 1), :].rearrange("p t h -> p (t h)").unsqueeze(2).broadcast_to([P, H, dh]),
                                        ALU.mult).then_inc(em_ready, 1)

            def rest(t, k):
                dve.wait_ge(part_done, t + 1)
                nc.vector.tensor_tensor(emx_cols(t, 1), flat(em[:, k]), emx_cols(t, 0), ALU.subtract).then_inc(rest_done, 1)

            def e_columns(n):
                e = e_all[:, ds(n * CT, CT), :].rearrange("p t (g h) -> p t g h", g=2)
                high_part, low_part = (emx[:, ds(n * CT, CT), q, :].rearrange("p t (g v) -> p t g v", g=2)[:, :, :, V:sh.GC] for q in range(2))
                nc.vector.tensor_copy(high_part, e).then_inc(e_high, 1)
                dve.wait_ge(e_high, n + 1)
                nc.vector.tensor_tensor(low_part, e, high_part, ALU.subtract)

            def step(i, first, last):
                for kc in range(2):
                    n = 2 * i + kc
                    more = not (last and kc == 1)
                    before = emx is not None and not (first and kc == 0)
                    for m in range(CT):
                        t, k = CT * n + m, m % 2
                        if more or m < CT - 1:
                            low(t + 1, 1 - k)
                        if m == 0 and before:
                            t_less_shift(n - 1)
                        if before:
                            if not (first and kc == 1 and m == 0):
                                rest(t - CT - 1, 1 - k)
                            if m == 0:
                                dve.wait_ge(e_ready, n)
                            weigh(t - CT, k)
                        at = CT * kc + m
                        late = first and not last
                        if late and at < SPREAD:
                            left = NT - 2 * CT
                            statistics(range(2 * CT + left * at // SPREAD, 2 * CT + left * (at + 1) // SPREAD))
                        if late and at == SPREAD - 1:
                            moments(2)
                        if m == CT - 1 and before:
                            e_columns(n - 1)
                        dve.wait_ge(projected, t + 3)
                        nc.vector.tensor_scalar(t_all[:, ds(t, 1), :], psE[:, k:k + 1, 0:H], 1.0 / W_SCALE, None, ALU.mult).then_inc(t_done, 1)
                        if late and at == SPREAD - 1:
                            norms(2)
                        if first and kc == 0 and m == CT - 1 and emx is not None:
                            dve.wait_ge(t_done, CT + 2)
                            nc.vector.tensor_reduce(tmax[:], t_all[:, 0:CT, :].rearrange("p t h -> p h t"), op=ALU.max, axis=AX_X).then_inc(tmax_ready, 1)

            def first_norms(b):
                statistics(BATCHES[b])
                moments(b)
                norms(b)

            first_norms(0)
            dve.wait_ge(w_hi, 1)
            nc.vector.scalar_tensor_tensor(w16[:, 1, :, 0:D], w[:], W_SCALE, w16[:, 0, :, 0:D], ALU.mult, ALU.subtract).then_inc(w_ready, 1)
            low(0, 0)
            dve.wait_ge(adst_in, 16)
            link = Chain(dve, w_chain)
            link(nc.vector.tensor_tensor(wprod[:], w[:], adst[:].unsqueeze(1).broadcast_to([P, DC, D]), ALU.mult))
            link(nc.vector.tensor_reduce(wt[:], wprod[:].rearrange("p c (h d) -> p c h d", h=H), op=ALU.add, axis=AX_X))
            link(nc.vector.tensor_scalar(w16[:, 0, :, D:DH], wt[:], W_SCALE, None, ALU.mult))
            nc.vector.scalar_tensor_tensor(w16[:, 1, :, D:DH], wt[:], W_SCALE, w16[:, 0, :, D:DH], ALU.mult, ALU.subtract).then_inc(w_ready, 1)
            first_norms(1)
            chunk_pairs(dve, step)
            if emx is not None:
                t_less_shift(NC - 1)
                if NC > 1:
                    rest(NT - CT - 1, 1)
                dve.wait_ge(e_ready, NC)
                for m in range(CT):
                    weigh(NT - CT + m, m % 2)
                    if m > 0:
                        rest(NT - CT + m - 1, 1 - m % 2)
                e_columns(NC - 1)
                rest(NT - 1, 1)


def gat_attention(nc, sh, x, adj, emx, mv1, maskD, x1D, flag, c):
    NT, H, dh, HG, N = sh.NT, sh.H, sh.dh, sh.HG, sh.N
    TG = 8
    NG = NT // TG if NT >= TG else 1
    TG = NT // NG
    with ExitStack() as ctx:
        s = Scope(nc, ctx, "ga")
        rows = s.sb("rows", [P, 2, N], F32)
        rows01 = s.sb("rows01", [P, 2, N], BF16)
        colsT = s.sb("colsT", [P, 2, N], BF16)
        mask = s.sb("mask", [P, 2, N], F16)
        xt = s.sb("xt", [P, 2, sh.D], F32)
        x1 = s.sb("x1", [P, 2, sh.D], F32)
        rsum = s.sb("rsum", [P, NT, 2, HG], F32)
        good = s.sb("good", [P, NT * (H + 1)], F32)
        bad = s.sb("bad", [P, 3], F32)
        stats = s.sb("stats", [P, 2, 6], F32)
        pair = s.sb("pair", [P, 2, 2], F32)
        psT = s.ps("psT", [P, 4, 1024], BF16)
        psO = s.ps("psO", [P, 2, 2, 512])

        rows_in = [s.sem(f"rows_in{k}") for k in range(2)]
        x_in = [s.sem(f"x_in{k}") for k in range(2)]
        cast = s.sem("cast")
        turned = s.sem("turned")
        cols_ready = s.sem("cols_ready")
        summed = s.sem("summed")
        masked = s.sem("masked")
        x1_ready = s.sem("x1_ready")
        mask_out = [s.sem(f"mask_out{k}") for k in range(2)]
        x1_out = [s.sem(f"x1_out{k}") for k in range(2)]
        stats_done = s.sem("stats_done")
        chain = s.sem("chain")
        raised = s.sem("raised")
        bad_ready = s.sem("bad_ready")
        bad_spread = s.sem("bad_spread")
        waited = s.sem("waited")
        block = s.block()

        @block.sync
        def _(sp):
            for k in range(2):
                sp.dma_start(rows[:, k, :], adj[k * P:(k + 1) * P, :]).then_inc(rows_in[k], 16)
            for k in range(2):
                sp.sem_inc(mask_out[k], 16)
                sp.sem_inc(x1_out[k], 16)

            def step(i, last):
                for k in range(2):
                    t = 2 * i + k
                    sp.wait_ge(x1_ready, t + 1)
                    sp.dma_start(xt[:, k, :], x[ds(t * P, P), :]).then_inc(x_in[k], 16)
                    if not last:
                        sp.wait_ge(cast, t + 1)
                        sp.dma_start(rows[:, k, :], adj[ds((t + 2) * P, P), :]).then_inc(rows_in[k], 16)
                    sp.wait_ge(masked, t + 3)
                    sp.dma_start(maskD[ds(t, 1)].rearrange("o p n -> (o p) n"), mask[:, k, :]).then_inc(mask_out[k], 16)
                    sp.wait_ge(x1_ready, t + 3)
                    sp.dma_start(x1D[ds(t * P, P), :], x1[:, k, :]).then_inc(x1_out[k], 16)

            in_pairs(sp, NT // 2, step)
            for k in range(2):
                sp.wait_ge(mask_out[k], 16 * (NT // 2) + 16)
                sp.wait_ge(x1_out[k], 16 * (NT // 2) + 16)

        @block.tensor
        def _(pe):
            pe.sem_inc(turned, 2 * NG)
            pe.sem_inc(summed, 2)

            def turn(t, k):
                pe.wait_ge(cast, t + 1)
                for g in range(NG):
                    pe.wait_ge(cols_ready, NG * t + g + 1)
                    for j in range(TG):
                        col = (g * TG + j) * P
                        last = nc.tensor.transpose(psT[:, g, j * P:(j + 1) * P], rows01[:, k, col:col + P], c.ident_bf[:])
                    last.then_inc(turned, 1)

            def step(i, last):
                for k in range(2):
                    t = 2 * i + k
                    if not (last and k == 1):
                        turn(t + 1, 1 - k)
                    pe.wait_ge(cols_ready, NG * t + 2 * NG)
                    pe.wait_ge(x1_ready, t + 1)
                    for j in range(NT):
                        for g in range(2):
                            for q in range(2):
                                mm = nc.tensor.matmul(psO[:, k, g, 0:sh.GC], colsT[:, k, j * P:(j + 1) * P],
                                                      emx[:, j, q, g * sh.GC:(g + 1) * sh.GC],
                                                      start=j == 0 and q == 0, stop=j == NT - 1 and q == 1)
                    mm.then_inc(summed, 1)

            turn(0, 0)
            in_pairs(pe, NT // 2, step)

        @block.scalar
        def _(act):
            act.sem_inc(cols_ready, NG)

            def step(i, last):
                for k in range(2):
                    t = 2 * i + k
                    act.wait_ge(summed, t + 1)
                    act.wait_ge(masked, t + 1)
                    for g in range(NG):
                        act.wait_ge(turned, NG * t + 2 * NG + g + 1)
                        nc.scalar.activation(colsT[:, k, g * TG * P:(g + 1) * TG * P], psT[:, g, 0:TG * P], ACT.Copy).then_inc(cols_ready, 1)

            in_pairs(act, NT // 2, step)

        @block.vector
        def _(dve):
            dve.sem_inc(masked, 2)
            dve.sem_inc(x1_ready, 2)
            dve.sem_inc(stats_done, 2)

            def cast_rows(t, k):
                dve.wait_ge(rows_in[k], (t - k) * 8 + 16)
                dve.wait_ge(turned, NG * t + NG)
                nc.vector.tensor_scalar(rows01[:, k, :], rows[:, k, :], 0.0, None, ALU.is_gt).then_inc(cast, 1)

            def make_mask(t, k):
                dve.wait_ge(cols_ready, NG * t + 2 * NG)
                dve.wait_ge(mask_out[k], (t - k) * 8 + 16)
                nc.vector.tensor_scalar(mask[:, k, :], colsT[:, k, :], -MASKED, MASKED, ALU.mult, ALU.add).then_inc(raised, 1)
                dve.wait_ge(raised, t + 1)
                diag = mask[:, k, ds(t * P, P)]
                nc.vector.tensor_tensor(diag, diag, c.diag_mask[:], ALU.max).then_inc(masked, 1)

            STEPS = 4

            def finish(t, k):
                link = Chain(dve, chain, STEPS * t)
                dve.wait_ge(summed, t + 3)
                sums = psO[:, k, :, HG * dh:sh.GC]
                rs = rsum[:, ds(t, 1)].rearrange("p o g h -> p (o g) h")
                link(nc.vector.reciprocal(rs, sums))
                dve.wait_ge(x1_out[k], (t - k) * 8 + 16)
                link(nc.vector.tensor_tensor(x1[:, k, :].rearrange("p (g h d) -> p g h d", g=2, h=HG),
                                             psO[:, k, :, 0:HG * dh].rearrange("p g (h d) -> p g h d", h=HG),
                                             rs.unsqueeze(3).broadcast_to([P, 2, HG, dh]), ALU.mult))
                dve.wait_ge(x_in[k], (t - k) * 8 + 16)
                nc.vector.tensor_tensor(x1[:, k, :], x1[:, k, :], xt[:, k, :], ALU.add).then_inc(x1_ready, 1)
                dve.wait_ge(x1_ready, t + 3)
                link(nc.vector.bn_stats(stats[:, k, :], x1[:, k, :]))
                dve.sem_inc(waited, 1)
                link(nc.vector.bn_aggr(pair[:, k, :], stats[:, k, :]))
                nc.vector.tensor_copy(mv1[:, ds(t, 1), :], pair[:, k:k + 1, :]).then_inc(stats_done, 1)
                assert link.n == STEPS

            def step(i, last):
                for k in range(2):
                    t = 2 * i + k
                    if not last:
                        cast_rows(t + 2, k)
                    if not (last and k == 1):
                        make_mask(t + 1, 1 - k)
                    finish(t, k)

            cast_rows(0, 0)
            cast_rows(1, 1)
            make_mask(0, 0)
            in_pairs(dve, NT // 2, step)
            dve.wait_ge(stats_done, NT + 2)
            link = Chain(dve, chain, STEPS * NT)
            link(nc.vector.tensor_scalar(good[:, 0:NT * H], rsum[:].rearrange("p t g h -> p (t g h)"), 256.0 / E_MOST, None, ALU.is_le))
            link(nc.vector.tensor_scalar(good[:, NT * H:], mv1[:, :, 1], 1e30, None, ALU.is_lt))
            raise_flag(nc, dve, link, good[:], bad, flag, bad_ready, bad_spread)

        @block.gpsimd
        def _(pool):
            spread_bad(nc, pool, bad, bad_ready, bad_spread)


def scores_for_attention(nc, sh, xm, t_all, d, c):
    NT, H, dh, D, N, VC = sh.NT, sh.H, sh.dh, sh.D, sh.N, sh.VC
    NCB = -(-H * NT // P)
    CB = H * NT // NCB
    FILLS = 4 * (D // P)
    with ExitStack() as ctx:
        s = Scope(nc, ctx, "form")
        zero = s.sb("zero", [P, N], F16)
        unit = s.sb("unit", [H, N], F16)
        t_cols = s.sb("t_cols", [P, H, NT], F32)
        part = s.sb("part", [P, NCB, 2, P], F16)
        v = s.sb("v", [P, 2, H, VC], F16)
        ps = s.ps("ps", [P, NCB, 512])
        set_ = s.sem("set")
        filled = s.sem("filled")
        rows_out = s.sem("rows_out")
        t_ready = s.sem("t_ready")
        turned = s.sem("turned")
        high_done = s.sem("high_done")
        parts_ready = s.sem("parts_ready")
        t_out = s.sem("t_out")
        v_high = s.sem("v_high")
        v_ready = s.sem("v_ready")
        v_out = [s.sem(f"v_out{k}") for k in range(2)]
        block = s.block()

        def first_rows(a):
            return a.rearrange("(h d) n -> d h n", h=H)[0]

        @block.sync
        def _(sp):
            sp.wait_ge(set_, 3)
            for a in (d.qhi, d.qlo, d.khi, d.klo):
                for r in range(D // P):
                    sp.dma_start(a[r * P:(r + 1) * P, :], zero[:]).then_inc(filled, 16)
            for b in range(NCB):
                sp.wait_ge(parts_ready, b + 1)
                for q, a in enumerate((d.t_hi, d.t_lo)):
                    sp.dma_start(a.rearrange("h (t p) -> (h t) p", p=P)[b * CB:(b + 1) * CB, :], part[0:CB, b, q, :]).then_inc(t_out, 16)
            sp.wait_ge(filled, 16 * FILLS)
            sp.wait_ge(t_out, 16 * 2 * NCB)
            for to, of in ((d.qhi, unit[:]), (d.khi, d.t_hi), (d.klo, d.t_lo)):
                sp.dma_start(first_rows(to), of).then_inc(rows_out, 16)
            sp.wait_ge(rows_out, 16 * 3)

        @block.gpsimd
        def _(pool):
            nc.gpsimd.memset(zero[:], 0.0).then_inc(set_, 1)
            nc.gpsimd.memset(unit[:], W_SCALE * float(dh) ** 0.5).then_inc(set_, 1)
            nc.gpsimd.memset(v[:, :, :, dh:dh + 1], 1.0).then_inc(set_, 1)

        @block.tensor
        def _(pe):
            pe.wait_ge(t_ready, 1)
            for b in range(NCB):
                nc.tensor.transpose(ps[0:CB, b, 0:P], t_cols[:].rearrange("p h t -> p (h t)")[:, b * CB:(b + 1) * CB], c.ident[:]).then_inc(turned, 1)

        @block.scalar
        def _(act):
            for k in range(2):
                act.sem_inc(v_out[k], 16)
            act.wait_ge(set_, 3)

            def store(n, k):
                act.wait_ge(v_ready, n + 1)
                act.sem_inc(v_high, 1)
                act.dma_start(d.v[:, :, ds(n * VC, VC)].rearrange("h p c -> p h c"), v[:, k]).then_inc(v_out[k], 16)

            with act.Fori(0, NT // 2) as i:
                for k in range(2):
                    n = 2 * i + k
                    act.wait_ge(v_out[k], 16 * i + 16)
                    nc.scalar.activation(v[:, k, :, 0:dh], xm[:, ds(n, 1), :].rearrange("p o (h d) -> p (o h) d", h=H), ACT.Copy).then_inc(v_high, 1)
                    store(n, k)
            for k in range(2):
                act.wait_ge(v_out[k], 16 * (NT // 2) + 16)

        @block.vector
        def _(dve):
            nc.vector.tensor_copy(t_cols[:], t_all[:].rearrange("p t h -> p h t")).then_inc(t_ready, 1)
            for b in range(NCB):
                dve.wait_ge(turned, b + 1)
                nc.vector.tensor_copy(part[0:CB, b, 0, :], ps[0:CB, b, 0:P]).then_inc(high_done, 1)
                dve.wait_ge(high_done, b + 1)
                nc.vector.tensor_tensor(part[0:CB, b, 1, :], ps[0:CB, b, 0:P], part[0:CB, b, 0, :], ALU.subtract).then_inc(parts_ready, 1)
            with dve.Fori(0, NT // 2) as i:
                for k in range(2):
                    n = 2 * i + k
                    dve.wait_ge(v_high, 2 * n + 1)
                    nc.vector.tensor_tensor(v[:, k, :, dh + 1:VC], xm[:, ds(n, 1), :].rearrange("p o (h d) -> p (o h) d", h=H), v[:, k, :, 0:dh], ALU.subtract).then_inc(v_ready, 1)


def plain_masks(nc, sh, adj, maskD, c):
    NT, N = sh.NT, sh.N
    TG = min(8, NT)
    NG = NT // TG
    with ExitStack() as ctx:
        s = Scope(nc, ctx, "pm")
        rows = s.sb("rows", [P, 2, N], F32)
        rows01 = s.sb("rows01", [P, N], BF16)
        mask = s.sb("mask", [P, 2, N], F16)
        psT = s.ps("psT", [P, NG, 1024], BF16)
        rows_in = [s.sem(f"rows_in{k}") for k in range(2)]
        cast = s.sem("cast")
        rows_free = s.sem("rows_free")
        turned = s.sem("turned")
        masked = s.sem("masked")
        mask_out = [s.sem(f"mask_out{k}") for k in range(2)]
        waited = s.sem("waited")
        block = s.block()

        @block.sync
        def _(sp):
            for k in range(2):
                sp.sem_inc(mask_out[k], 16)
            with sp.Fori(0, NT // 2) as i:
                for k in range(2):
                    t = 2 * i + k
                    sp.wait_ge(rows_free, t + 1)
                    sp.sem_inc(waited, 1)
                    sp.dma_start(rows[:, k, :], adj[ds(t * P, P), :]).then_inc(rows_in[k], 16)
                    sp.wait_ge(masked, t + 2)
                    sp.sem_inc(waited, 1)
                    sp.dma_start(maskD[ds(t, 1)].rearrange("o p n -> (o p) n"), mask[:, k, :]).then_inc(mask_out[k], 16)
            for k in range(2):
                sp.wait_ge(mask_out[k], 16 * (NT // 2) + 16)

        @block.tensor
        def _(pe):
            pe.sem_inc(turned, 1)
            with pe.Fori(0, NT) as t:
                pe.wait_ge(cast, t + 1)
                pe.wait_ge(masked, t + 1)
                for j in range(NT):
                    last = nc.tensor.transpose(psT[:, j // TG, (j % TG) * P:(j % TG + 1) * P], rows01[:, j * P:(j + 1) * P], c.ident_bf[:])
                last.then_inc(turned, 1)

        @block.vector
        def _(dve):
            dve.sem_inc(rows_free, 2)
            dve.sem_inc(masked, 1)
            with dve.Fori(0, NT // 2) as i:
                for k in range(2):
                    t = 2 * i + k
                    dve.wait_ge(rows_in[k], 16 * i + 16)
                    dve.wait_ge(turned, t + 1)
                    nc.vector.tensor_scalar(rows01[:], rows[:, k, :], 0.0, None, ALU.is_gt).then_inc(cast, 1)
                    dve.wait_ge(cast, t + 1)
                    dve.sem_inc(rows_free, 1)
                    dve.wait_ge(turned, t + 2)
                    dve.wait_ge(mask_out[k], 16 * i + 16)
                    nc.vector.tensor_scalar(mask[:, k, :].rearrange("p (g n) -> p g n", g=NG), psT[:, :, 0:TG * P], -MASKED, MASKED,
                                            ALU.mult, ALU.add).then_inc(masked, 1)


def add_residual(nc, sh, x, d, mv1, x1D):
    NT, D = sh.NT, sh.D
    STEPS = 4
    with ExitStack() as ctx:
        s = Scope(nc, ctx, "res")
        xt = s.sb("xt", [P, 2, D], F32)
        at = s.sb("at", [P, 2, D], F32)
        x1 = s.sb("x1", [P, 2, D], F32)
        stats = s.sb("stats", [P, 6], F32)
        pair = s.sb("pair", [P, 2], F32)
        tile_in = [s.sem(f"tile_in{k}") for k in range(2)]
        tile_done = s.sem("tile_done")
        x1_out = [s.sem(f"x1_out{k}") for k in range(2)]
        chain = s.sem("chain")
        waited = s.sem("waited")
        block = s.block()

        @block.sync
        def _(sp):
            for k in range(2):
                sp.sem_inc(x1_out[k], 16)
                sp.dma_start(xt[:, k, :], x[k * P:(k + 1) * P, :]).then_inc(tile_in[k], 16)
                sp.dma_start(at[:, k, :], d.att[k * P:(k + 1) * P, :]).then_inc(tile_in[k], 16)

            def step(i, last):
                for k in range(2):
                    t = 2 * i + k
                    sp.wait_ge(tile_done, t + 3)
                    sp.sem_inc(waited, 1)
                    sp.dma_start(x1D[ds(t * P, P), :], x1[:, k, :]).then_inc(x1_out[k], 16)
                    if not last:
                        sp.dma_start(xt[:, k, :], x[ds((t + 2) * P, P), :]).then_inc(tile_in[k], 16)
                        sp.dma_start(at[:, k, :], d.att[ds((t + 2) * P, P), :]).then_inc(tile_in[k], 16)

            in_pairs(sp, NT // 2, step)
            for k in range(2):
                sp.wait_ge(x1_out[k], 16 * (NT // 2) + 16)

        @block.vector
        def _(dve):
            dve.sem_inc(tile_done, 2)
            with dve.Fori(0, NT // 2) as i:
                for k in range(2):
                    t = 2 * i + k
                    link = Chain(dve, chain, STEPS * t)
                    dve.wait_ge(tile_in[k], 32 * i + 32)
                    dve.wait_ge(x1_out[k], 16 * i + 16)
                    link(nc.vector.tensor_tensor(x1[:, k, :], xt[:, k, :], at[:, k, :], ALU.add))
                    link(nc.vector.bn_stats(stats[:], x1[:, k, :]))
                    dve.sem_inc(waited, 1)
                    link(nc.vector.bn_aggr(pair[:], stats[:]))
                    link(nc.vector.tensor_copy(mv1[:, ds(t, 1), :], pair[:].unsqueeze(1)))
                    dve.sem_inc(tile_done, 1)


def qkv(nc, sh, x1D, wq, wk, wv, wo, wo16, mv1, d, c):
    NT, DC, H, dh, D, VC = sh.NT, sh.DC, sh.H, sh.dh, sh.D, sh.VC
    GT = 4
    NGR = NT // GT
    OUTS = 2 * DC + GT
    with ExitStack() as ctx:
        s = Scope(nc, ctx, "qkv")
        w = s.sb("w", [P, 3, DC, D], F32)
        wo32 = s.sb("wo32", [P, DC, D], F32)
        w16 = s.sb("w16", [P, 3, 2, DC, D], F16)
        xt = s.sb("xt", [P, 2, GT, D], F32)
        h = s.sb("h", [P, 2, GT, D], F32)
        hT = s.sb("hT", [P, 2, DC, 2, GT * P], F16)
        hi = s.sb("hi", [P, 2, 2 * DC, 512], F16)
        lo = s.sb("lo", [P, 2, 2 * DC, 512], F16)
        v = s.sb("v", [P, 2, H, GT, VC], F16)
        sum0 = s.sb("sum0", [P, DC], F32)
        off = s.sb("off", [P, DC], F32)
        rstd = s.sb("rstd", [P, NT], F32)
        shift = s.sb("shift", [P, NT], F32)
        eps = s.sb("eps", [P, 1], F32)
        psT = s.ps("psT", [P, 2, 512])
        psP = s.ps("psP", [P, 4, 512])

        w_in = [s.sem(f"w_in{n}") for n in range(3)]
        wo_in = s.sem("wo_in")
        x_in = [s.sem(f"x_in{k}") for k in range(2)]
        eps_set = s.sem("eps_set")
        std_done = s.sem("std_done")
        chain = s.sem("chain")
        w_hi = s.sem("w_hi")
        w_ready = s.sem("w_ready")
        norm_ready = s.sem("norm_ready")
        ones_set = s.sem("ones_set")
        h_ready = s.sem("h_ready")
        turned = s.sem("turned")
        hT_hi = s.sem("hT_hi")
        hT_ready = s.sem("hT_ready")
        projected = s.sem("projected")
        waited = s.sem("waited")
        hi_ready = s.sem("hi_ready")
        lo_ready = s.sem("lo_ready")
        first_keys = s.sem("first_keys")
        off_ready = s.sem("off_ready")
        parts_out = [s.sem(f"parts_out{k}") for k in range(2)]
        OUT_INC = 16 * (4 * DC + H)
        block = s.block()

        @block.gpsimd
        def _(pool):
            def load_x(t, k):
                pool.dma_start(xt[:, k], x1D[ds(t * (GT * P), GT * P), :].rearrange("(t p) d -> p t d", p=P)).then_inc(x_in[k], 16)

            def load_weights(n, m):
                for k in range(DC):
                    pool.dma_start(w[:, n, k, :].rearrange("p (h d) -> p h d", h=H),
                                   m[:, k * P:(k + 1) * P, :].rearrange("h p d -> p h d")).then_inc(w_in[n], 16)

            load_x(0, 0)
            load_weights(1, wk)
            load_weights(0, wq)
            load_x(1, 1)
            load_weights(2, wv)
            pool.dma_start(wo32[:], wo.rearrange("h k o -> (h k) o").rearrange("(c p) o -> p c o", p=P)).then_inc(wo_in, 16)
            if NGR > 2:
                with pool.Fori(1, NGR // 2) as i:
                    for k in range(2):
                        t = 2 * i + k
                        pool.wait_ge(h_ready, t + 1)
                        load_x(t, k)

        @block.sync
        def _(sp):
            for k in range(2):
                sp.sem_inc(parts_out[k], OUT_INC)

            with sp.Fori(0, NGR // 2) as i:
                for k in range(2):
                    t = 2 * i + k
                    tok = ds(t * (GT * P), GT * P)
                    for n in range(2 * DC):
                        hiD, loD = (d.qhi, d.qlo) if n < DC else (d.khi, d.klo)
                        r = (n % DC) * P
                        sp.wait_ge(lo_ready, OUTS * t + n + 5)
                        if n == 0:
                            sp.sem_inc(waited, 1)
                        sp.dma_start(hiD[r:r + P, tok], hi[:, k, n, :]).then_inc(parts_out[k], 16)
                        sp.dma_start(loD[r:r + P, tok], lo[:, k, n, :]).then_inc(parts_out[k], 16)
                    sp.wait_ge(lo_ready, OUTS * t + OUTS + 4)
                    sp.sem_inc(waited, 1)
                    for hh in range(H):
                        sp.dma_start(d.v[hh, :, ds(t * GT * VC, GT * VC)], v[:, k, hh].rearrange("p t c -> p (t c)")).then_inc(parts_out[k], 16)
            for k in range(2):
                sp.wait_ge(parts_out[k], OUT_INC * (NGR // 2 + 1))

        @block.tensor
        def _(pe):
            pe.sem_inc(turned, 2 * DC)
            pe.sem_inc(projected, 2 * OUTS)

            def turn(t, k):
                pe.wait_ge(h_ready, t + 3)
                for j in range(DC):
                    pe.wait_ge(hT_ready, DC * t + j + 1)
                    for g in range(GT):
                        tr = nc.tensor.transpose(psT[:, j % 2, g * P:(g + 1) * P], h[:, k, g, j * P:(j + 1) * P], c.ident[:])
                    tr.then_inc(turned, 1)

            def step(i, last):
                for k in range(2):
                    t = 2 * i + k
                    if not (last and k == 1):
                        turn(t + 1, 1 - k)
                    pe.wait_ge(hT_ready, DC * t + DC + 2)
                    for n in range(OUTS):
                        pe.wait_ge(lo_ready, OUTS * t + n + 1)
                        if n < 2 * DC:
                            r = (n % DC) * P
                            chunks = [(w16[:, n // DC, :, j, r:r + P], hT[:, k, j]) for j in range(DC)]
                        else:
                            g = n - 2 * DC
                            chunks = [(hT[:, k, j, :, g * P:(g + 1) * P], w16[:, 2, :, j, :]) for j in range(DC)]
                        split_matmuls(nc, psP[:, n % 4, :], chunks).then_inc(projected, 1)

            turn(0, 0)
            pe.wait_ge(w_ready, 1)
            pe.wait_ge(hT_ready, DC + 2)
            for n in range(DC):
                mm = split_matmuls(nc, psP[:, n, 0:P], [(w16[:, 1, :, j, n * P:(n + 1) * P], hT[:, 0, j, :, 0:P]) for j in range(DC)])
            mm.then_inc(first_keys, 1)
            pe.wait_ge(off_ready, 1)
            pe.wait_ge(w_ready, 3)
            in_pairs(pe, NGR // 2, step)

        @block.scalar
        def _(act):
            act.sem_inc(h_ready, 2)
            act.wait_ge(eps_set, 1)
            nc.scalar.activation(rstd[:], mv1[:, :, 1], ACT.Sqrt, bias=eps[:]).then_inc(std_done, 1)
            act.wait_ge(norm_ready, 1)

            def relu_norm(t, k):
                act.wait_ge(x_in[k], (t - k) * 8 + 16)
                act.wait_ge(turned, DC * t + DC)
                for g in range(GT):
                    r = nc.scalar.activation(h[:, k, g, :], xt[:, k, g, :], ACT.Relu, bias=shift[:, ds(t * GT + g, 1)],
                                             scale=rstd[:, ds(t * GT + g, 1)])
                r.then_inc(h_ready, 1)

            def high(t, k):
                act.wait_ge(projected, OUTS * t + OUTS)
                for j in range(DC):
                    act.wait_ge(turned, DC * t + 2 * DC + j + 1)
                    nc.scalar.activation(hT[:, k, j, 0, :], psT[:, j % 2, :], ACT.Copy).then_inc(hT_hi, 1)

            def step(i, last):
                for k in range(2):
                    t = 2 * i + k
                    if not (last and k == 1):
                        high(t + 1, 1 - k)
                    if not last:
                        relu_norm(t + 2, k)
                    act.wait_ge(parts_out[k], (t - k) * (OUT_INC // 2) + OUT_INC)
                    for n in range(OUTS):
                        act.wait_ge(projected, OUTS * t + 2 * OUTS + n + 1)
                        if n < 2 * DC:
                            to, of = hi[:, k, n, :], psP[:, n % 4, :]
                        else:
                            to = v[:, k, :, n - 2 * DC, 0:dh]
                            of = psP[:, n % 4, :].rearrange("p (h d) -> p h d", h=H)
                        if DC <= n < 2 * DC:
                            ins = nc.scalar.activation(to, of, ACT.Identity, bias=off[:, n - DC:n - DC + 1])
                        else:
                            ins = nc.scalar.activation(to, of, ACT.Copy, scale=1.0 / W_SCALE)
                        ins.then_inc(hi_ready, 1)

            def high_weights(n):
                act.wait_ge(w_in[n], 16 * DC)
                nc.scalar.activation(w16[:, n, 0], w[:, n], ACT.Copy, scale=W_SCALE).then_inc(w_hi, 1)

            relu_norm(0, 0)
            high_weights(1)
            high(0, 0)
            high_weights(0)
            relu_norm(1, 1)
            high_weights(2)
            act.wait_ge(off_ready, 1)
            in_pairs(act, NGR // 2, step)
            act.wait_ge(wo_in, 16)
            nc.scalar.activation(wo16[:, :, 0, :], wo32[:], ACT.Copy, scale=W_SCALE).then_inc(w_hi, 1)

        @block.vector
        def _(dve):
            dve.sem_inc(hT_ready, 2)
            dve.sem_inc(lo_ready, 4)
            nc.vector.memset(eps[:], EPS).then_inc(eps_set, 1)
            nc.vector.memset(v[:, :, :, :, dh:dh + 1], 1.0).then_inc(ones_set, 1)
            dve.wait_ge(std_done, 1)
            link = Chain(dve, chain)
            link(nc.vector.reciprocal(rstd[:], rstd[:]))
            nc.vector.scalar_tensor_tensor(shift[:], mv1[:, :, 0], -1.0, rstd[:], ALU.mult, ALU.mult).then_inc(norm_ready, 1)
            dve.wait_ge(ones_set, 1)

            def low_T(t, k):
                for j in range(DC):
                    dve.wait_ge(hT_hi, DC * t + j + 1)
                    nc.vector.tensor_tensor(hT[:, k, j, 1, :], psT[:, j % 2, :], hT[:, k, j, 0, :], ALU.subtract).then_inc(hT_ready, 1)

            def step(i, last):
                for k in range(2):
                    t = 2 * i + k
                    if not (last and k == 1):
                        low_T(t + 1, 1 - k)
                    for n in range(OUTS):
                        dve.wait_ge(hi_ready, OUTS * t + n + 1)
                        if n < 2 * DC:
                            to, of, high = lo[:, k, n, :], psP[:, n % 4, :], hi[:, k, n, :]
                        else:
                            g = n - 2 * DC
                            to, high = v[:, k, :, g, dh + 1:VC], v[:, k, :, g, 0:dh]
                            of = psP[:, n % 4, :].rearrange("p (h d) -> p h d", h=H)
                        if DC <= n < 2 * DC:
                            ins = nc.vector.scalar_tensor_tensor(to, of, off[:, n - DC:n - DC + 1], high, ALU.add, ALU.subtract)
                        else:
                            ins = nc.vector.scalar_tensor_tensor(to, of, 1.0 / W_SCALE, high, ALU.mult, ALU.subtract)
                        ins.then_inc(lo_ready, 1)

            def low_weights(n, m):
                dve.wait_ge(w_hi, m + 1)
                nc.vector.scalar_tensor_tensor(w16[:, n, 1], w[:, n], W_SCALE, w16[:, n, 0], ALU.mult, ALU.subtract).then_inc(w_ready, 1)

            low_weights(1, 0)
            low_T(0, 0)
            low_weights(0, 1)
            dve.wait_ge(first_keys, 1)
            link(nc.vector.tensor_reduce(sum0[:], psP[:, :, 0:P], op=ALU.add, axis=AX_X))
            nc.vector.tensor_scalar(off[:], sum0[:], -1.0 / P, None, ALU.mult).then_inc(off_ready, 1)
            low_weights(2, 2)
            dve.wait_ge(off_ready, 1)
            in_pairs(dve, NGR // 2, step)
            dve.wait_ge(w_hi, 4)
            nc.vector.scalar_tensor_tensor(wo16[:, :, 1, :], wo32[:], W_SCALE, wo16[:, :, 0, :], ALU.mult, ALU.subtract)


def row_maxima(nc, sh, adj, d, c, tag, own):
    NT, H, dh, N = sh.NT, sh.H, sh.dh, sh.N
    KC = min(2048, N)
    NK = N // KC
    with ExitStack() as ctx:
        s = Scope(nc, ctx, tag)
        ks = s.sb("ks", [P, H, N], F16)
        qt = s.sb("qt", [P, 2, H, P], F16)
        rows = s.sb("rows", [P, 2, N], F32)
        mask = s.sb("mask", [P, 2, N], BF16)
        junk = s.sb("junk", [P, 2, KC], BF16)
        part = s.sb("part", [P, 2, H, NK], F32)
        top = s.sb("top", [P, H, NT], F32)
        topT = s.sb("topT", [P, 2, P], F16)
        ps = s.ps("ps", [P, 2, KC])

        keys_in = s.sem("keys_in")
        q_in = [s.sem(f"q_in{k}") for k in range(2)]
        rows_in = [s.sem(f"rows_in{k}") for k in range(2)]
        mask_ready = s.sem("mask_ready")
        scored = s.sem("scored")
        reduced = s.sem("reduced")
        tile_done = s.sem("tile_done")
        diag_done = s.sem("diag_done")
        waited = s.sem("waited")
        turned = s.sem("turned")
        top_ready = s.sem("top_ready")
        top_out = s.sem("top_out")
        block = s.block()
        COLS = H * NT
        NCB = -(-COLS // P)
        CB = COLS // NCB

        @block.gpsimd
        def _(pool):
            for h in range(H):
                pool.dma_start(ks[0:dh, h, :], d.khi[h * dh:(h + 1) * dh, :]).then_inc(keys_in, 16)
                pool.dma_start(ks[dh:P, h, :], d.klo[h * dh:(h + 1) * dh, :]).then_inc(keys_in, 16)

        @block.sync
        def _(sp):
            with sp.Fori(0, NT // 2) as i:
                for k in range(2):
                    t = 2 * i + k
                    sp.wait_ge(mask_ready, t + 1)
                    sp.dma_start(rows[:, k, :], adj[ds(t * P, P), :]).then_inc(rows_in[k], 16)
                    sp.wait_ge(scored, (t + 1) * (H * NK))
                    sp.sem_inc(waited, 1)
                    src = d.qhi[:, ds(t * P, P)].rearrange("(h d) n -> d h n", h=H)
                    sp.dma_start(qt[0:dh, k], src).then_inc(q_in[k], 16)
                    sp.dma_start(qt[dh:P, k], src).then_inc(q_in[k], 16)
            for b in range(NCB):
                sp.wait_ge(top_ready, b + 1)
                sp.dma_start(d.shift.rearrange("h (t p) -> (h t) p", p=P)[b * CB:(b + 1) * CB, :], topT[0:CB, b, :]).then_inc(top_out, 16)
            sp.wait_ge(top_out, 16 * NCB)

        @block.scalar
        def _(act):
            act.sem_inc(mask_ready, 2)
            with act.Fori(0, NT // 2) as i:
                for k in range(2):
                    t = 2 * i + k
                    act.wait_ge(rows_in[k], 16 * i + 16)
                    act.wait_ge(tile_done, t + 1)
                    nc.scalar.activation(mask[:, k, :], rows[:, k, :], ACT.Copy, scale=-MASKED * W_SCALE, bias=MASKED * W_SCALE).then_inc(mask_ready, 1)

        @block.tensor
        def _(pe):
            pe.sem_inc(scored, 2 * H * NK)
            pe.wait_ge(keys_in, 16 * 2 * H)
            with pe.Fori(0, NT // 2) as i:
                for k in range(2):
                    t = 2 * i + k
                    pe.wait_ge(q_in[k], 32 * i + 32)
                    for h in range(H):
                        for m in range(NK):
                            n = h * NK + m
                            pe.wait_ge(reduced, t * (H * NK) + n + 1)
                            for j in range(KC // 512):
                                col = m * KC + j * 512
                                mm = nc.tensor.matmul(ps[:, n % 2, j * 512:(j + 1) * 512], qt[:, k, h, :],
                                                      ks[:, h, col:col + 512], start=True, stop=True)
                            mm.then_inc(scored, 1)
            pe.wait_ge(tile_done, NT + 2)
            for b in range(NCB):
                nc.tensor.transpose(ps[0:CB, b, 0:P], top[:].rearrange("p h t -> p (h t)")[:, b * CB:(b + 1) * CB], c.ident[:]).then_inc(turned, 1)

        @block.vector
        def _(dve):
            dve.sem_inc(reduced, 2)
            dve.sem_inc(tile_done, 2)
            with dve.Fori(0, NT // 2) as i:
                for k in range(2):
                    t = 2 * i + k
                    dve.wait_ge(mask_ready, t + 3)
                    if own:
                        diag = mask[:, k, ds(t * P, P)]
                        nc.vector.scalar_tensor_tensor(diag, c.diag_mask[:], W_SCALE, diag, ALU.mult, ALU.max).then_inc(diag_done, 1)
                        dve.wait_ge(diag_done, t + 1)
                    for n in range(H * NK):
                        dve.wait_ge(scored, (t + 2) * (H * NK) + n + 1)
                        dve.wait_ge(reduced, t * (H * NK) + n + 1)
                        dve.sem_inc(waited, 1)
                        m = n % NK
                        nc.vector.tensor_tensor_reduce(out=junk[:, n % 2, :], in0=ps[:, n % 2, :], in1=mask[:, k, m * KC:(m + 1) * KC],
                                                       scale=1.0, scalar=-3e38, op0=ALU.add, op1=ALU.max,
                                                       accum_out=part[:, k, n // NK, m:m + 1]).then_inc(reduced, 1)
                    dve.wait_ge(reduced, (t + 1) * (H * NK) + 2)
                    nc.vector.tensor_reduce(top[:, :, ds(t, 1)].rearrange("p h o -> p (h o)"), part[:, k], op=ALU.max, axis=AX_X).then_inc(tile_done, 1)
            for b in range(NCB):
                dve.wait_ge(turned, b + 1)
                nc.vector.tensor_scalar(topT[0:CB, b, :], ps[0:CB, b, 0:P], -1.0 / W_SCALE, None, ALU.mult).then_inc(top_ready, 1)


def attention(nc, sh, maskD, d, c, scale, tag, shifted, flag):
    NT, H, dh, N, VC, QB, QS = sh.NT, sh.H, sh.dh, sh.N, sh.VC, sh.QB, sh.QS
    HALF = QB // 512
    NI = sh.NB * H
    OB = 3
    NOB = -(-QS // OB)
    ITEM_INC = 16 * (7 if shifted else 6)
    assert HALF == 2
    NP = NT // 2
    MC = 4
    MP = NP // MC
    with ExitStack() as ctx:
        s = Scope(nc, ctx, tag)
        mask = s.sb("mask", [P, QS, NT * P], F16)
        ks = s.sb("ks", [P, 2, N], F16)
        v = s.sb("v", [P, 2, NT * VC], F16)
        qa = s.sb("qa", [P, 2, QB], F16)
        qb = s.sb("qb", [P, 2, QB], F16)
        qs = s.sb("qs", [1, 2, QB], F16)
        unit = s.sb("unit", [1, P], F16)
        e = s.sb("e", [P, 2, QB], F32)
        phi = s.sb("phi", [P, 2, QB], F16)
        plo = s.sb("plo", [P, 2, QB], F16)
        o = s.sb("o", [P, 2, QS, VC], F32)
        onum = s.sb("onum", [P, QS, dh], F32)
        oinv = s.sb("oinv", [P, NI, QS], F32)
        good = s.sb("good", [P, 2, NI * QS], F32)
        bad = s.sb("bad", [P, 3], F32)
        att = s.sb("att", [P, 2, QS, dh], F32)
        psS = s.ps("psS", [P, 2, QB])
        psO = s.ps("psO", [P, NOB, 512])

        ones_set = s.sem("ones_set")
        mask_in = [s.sem(f"mask_in{m}") for m in range(MC)]
        item_in = [s.sem(f"item_in{k}") for k in range(2)]
        v_in = [s.sem(f"v_in{k}") for k in range(2)]
        scored = s.sem("scored")
        exp_done = s.sem("exp_done")
        hi_done = s.sem("hi_done")
        lo_done = s.sem("lo_done")
        applied = s.sem("applied")
        bad_ready = s.sem("bad_ready")
        bad_spread = s.sem("bad_spread")
        o_copied = s.sem("o_copied")
        o_read = s.sem("o_read")
        att_ready = s.sem("att_ready")
        att_out = [s.sem(f"att_out{k}") for k in range(2)]
        chain = s.sem("chain")
        waited = s.sem("waited")
        block = s.block()

        @block.sync
        def _(sp):
            for k in range(2):
                sp.sem_inc(att_out[k], 16)

            def load(it, k):
                b, h = it // H, it % H
                qcols, hrows = ds(b * QB, QB), ds(h * dh, dh)
                parts = [(ks[0:dh, k, :], d.khi[hrows, :]), (ks[dh:P, k, :], d.klo[hrows, :])]
                parts += [(q[r:r + dh, k, :], of[hrows, qcols]) for q, of in ((qa, d.qhi), (qb, d.qlo)) for r in (0, dh)]
                if shifted:
                    parts.append((qs[:, k, :], d.shift[ds(h, 1), qcols]))
                for to, of in parts:
                    sp.dma_start(to, of).then_inc(item_in[k], 16)
                sp.dma_start(v[:, k, :], d.v[ds(h, 1)].rearrange("o p c -> (o p) c")).then_inc(v_in[k], 16)

            def step(i, last):
                for k in range(2):
                    it = 2 * i + k
                    b, h = it // H, it % H
                    sp.wait_ge(att_ready, it + 1)
                    sp.dma_start(d.att[ds(b * QB, QB), ds(h * dh, dh)].rearrange("(q p) d -> p q d", p=P), att[:, k]).then_inc(att_out[k], 16)
                    if not last:
                        load(it + 2, k)

            load(0, 0)
            sp.wait_ge(mask_in[0], 16)
            load(1, 1)
            in_pairs(sp, NI // 2, step)
            for k in range(2):
                sp.wait_ge(att_out[k], 16 * (NI // 2) + 16)

        @block.gpsimd
        def _(pool):
            def load_mask(b, m):
                cols = slice(m * 2 * MP * P, (m + 1) * 2 * MP * P)
                pool.dma_start(mask[:, :, cols], maskD[ds(b * QS, QS), :, cols].rearrange("q p n -> p q n")).then_inc(mask_in[m], 16)

            for m in range(MC):
                if m == 1:
                    pool.wait_ge(item_in[0], ITEM_INC)
                load_mask(0, m)
            if sh.NB > 1:
                with pool.Fori(1, sh.NB) as b:
                    for m in range(MC):
                        pool.wait_ge(scored, (b * H - 1) * NT + (m + 1) * 2 * MP)
                        load_mask(b, m)
            if flag is not None:
                spread_bad(nc, pool, bad, bad_ready, bad_spread)

        @block.tensor
        def _(pe):
            pe.sem_inc(applied, 2)
            if shifted:
                pe.wait_ge(ones_set, 1)

            def score(it, kt, par, k, first):
                g = it * NT + kt
                if not first:
                    pe.wait_ge(exp_done, g - 1)
                cols = ds(kt * P, P)
                halves = [slice(f * 512, (f + 1) * 512) for f in range(HALF)]
                for q in halves:
                    for part in (qa, qb):
                        nc.tensor.matmul(psS[:, par, q], ks[:, k, cols], part[:, k, q], start=part is qa, stop=False)
                    if shifted:
                        nc.tensor.matmul(psS[:, par, q], unit[:], qs[:, k, q], start=False, stop=False)
                for f, q in enumerate(halves):
                    mm = nc.tensor.matmul(psS[:, par, q].rearrange("p (q n) -> p q n", n=P), c.mask_ident[:],
                                          mask[:, f * 4:(f + 1) * 4, cols], start=False, stop=True)
                mm.then_inc(scored, 1)

            def apply(it, kt, par, k, first=False):
                g = it * NT + kt
                pe.wait_ge(lo_done, g + 3)
                for q in range(QS):
                    o_cols = psO[:, q // OB, (q % OB) * VC:(q % OB + 1) * VC]
                    qc = slice(q * P, (q + 1) * P)
                    nc.tensor.matmul(o_cols, phi[:, par, qc], v[:, k, ds(kt * VC, VC)], start=first and q % OB == 0, stop=False, skip_group_check=True)
                    mm = nc.tensor.matmul(o_cols[:, 0:dh + 1], plo[:, par, qc], v[:, k, ds(kt * VC, dh + 1)], start=False, stop=False, skip_group_check=True)
                return mm

            def begin(it, k):
                pe.wait_ge(item_in[k], (it - k) * (ITEM_INC // 2) + ITEM_INC)
                pe.wait_ge(mask_in[0], (it // H) * 16 + 16)

            def step(i, last):
                for k in range(2):
                    it = 2 * i + k
                    for m in range(MC):
                        if m > 0:
                            pe.wait_ge(mask_in[m], (it // H) * 16 + 16)
                            pe.sem_inc(waited, 1)
                        first, end = max(1, m * MP), (m + 1) * MP
                        if first == 1 and end > 1:
                            score(it, 2, 0, k, False)
                            if k == 1 or not isinstance(i, int) or i > 0:
                                pe.wait_ge(o_copied, it + 1)
                            pe.wait_ge(v_in[k], (it - k) * 8 + 16)
                            apply(it, 0, 0, k, True).then_inc(applied, 1)
                            score(it, 3, 1, k, False)
                            apply(it, 1, 1, k).then_inc(applied, 1)
                            first = 2
                        if first < end:
                            with pe.Fori(first, end) as j:
                                for n in range(2):
                                    score(it, 2 * j + n, n, k, False)
                                    apply(it, 2 * j + n - 2, n, k).then_inc(applied, 1)
                    more = not (last and k == 1)
                    if more:
                        begin(it + 1, 1 - k)
                        score(it + 1, 0, 0, 1 - k, False)
                    apply(it, NT - 2, 0, k).then_inc(applied, 1)
                    if more:
                        score(it + 1, 1, 1, 1 - k, False)
                    apply(it, NT - 1, 1, k).then_inc(applied, 1)

            begin(0, 0)
            score(0, 0, 0, 0, True)
            score(0, 1, 1, 0, True)
            in_pairs(pe, NI // 2, step)

        @block.scalar
        def _(act):
            act.sem_inc(o_copied, 1)

            def weigh(it, kt, par):
                g = it * NT + kt
                act.wait_ge(scored, g + 1)
                act.wait_ge(lo_done, g + 1)
                nc.scalar.activation(e[:, par, :], psS[:, par, :], ACT.Exp, scale=scale / W_SCALE).then_inc(exp_done, 1)

            def step(i, last):
                for k in range(2):
                    it = 2 * i + k
                    with act.Fori(1, NT // 2) as j:
                        for m in range(2):
                            weigh(it, 2 * j + m, m)
                    if not (last and k == 1):
                        weigh(it + 1, 0, 0)
                        weigh(it + 1, 1, 1)
                    act.wait_ge(applied, (it + 1) * NT + 2)
                    act.wait_ge(o_read, it + 1)
                    for b in range(NOB):
                        q0, q1 = b * OB, min(QS, b * OB + OB)
                        cp = nc.scalar.activation(o[:, k, q0:q1, :], psO[:, b, 0:(q1 - q0) * VC].rearrange("p (q c) -> p q c", c=VC), ACT.Copy)
                    cp.then_inc(o_copied, 1)

            weigh(0, 0, 0)
            weigh(0, 1, 1)
            in_pairs(act, NI // 2, step)

        @block.vector
        def _(dve):
            dve.sem_inc(lo_done, 2)
            dve.sem_inc(o_read, 2)
            if shifted:
                nc.vector.memset(unit[:], W_SCALE).then_inc(ones_set, 1)

            def split(it, kt, par):
                g = it * NT + kt
                dve.wait_ge(exp_done, g + 1)
                dve.wait_ge(applied, g + 1)
                nc.vector.tensor_copy(phi[:, par, :], e[:, par, :]).then_inc(hi_done, 1)
                dve.wait_ge(hi_done, g + 1)
                nc.vector.tensor_tensor(plo[:, par, :], e[:, par, :], phi[:, par, :], ALU.subtract).then_inc(lo_done, 1)

            STEPS = 1

            def step(i, last):
                for k in range(2):
                    it = 2 * i + k
                    with dve.Fori(1, NT // 2) as j:
                        for m in range(2):
                            split(it, 2 * j + m, m)
                    if not (last and k == 1):
                        split(it + 1, 0, 0)
                        split(it + 1, 1, 1)
                    dve.wait_ge(o_copied, it + 2)
                    inv = oinv[:, ds(it, 1), :].rearrange("p o q -> p (o q)")
                    nc.vector.reciprocal(inv, o[:, k, :, dh]).then_inc(chain, 1)
                    nc.vector.tensor_tensor(onum[:], o[:, k, :, 0:dh], o[:, k, :, dh + 1:VC], ALU.add).then_inc(o_read, 1)
                    dve.wait_ge(chain, it + 1)
                    dve.wait_ge(o_read, it + 3)
                    dve.wait_ge(att_out[k], (it - k) * 8 + 16)
                    nc.vector.tensor_tensor(att[:, k], onum[:], inv.unsqueeze(2).broadcast_to([P, QS, dh]), ALU.mult).then_inc(att_ready, 1)
                    dve.wait_ge(att_ready, it + 1)
                    dve.sem_inc(waited, 1)

            split(0, 0, 0)
            split(0, 1, 1)
            in_pairs(dve, NI // 2, step)
            if flag is not None:
                link = Chain(dve, chain, NI)
                of = oinv[:].rearrange("p i q -> p (i q)")
                link(nc.vector.tensor_scalar(good[:, 0, :], of, 16.0, None, ALU.is_le))
                link(nc.vector.tensor_scalar(good[:, 1, :], of, 0.0, None, ALU.is_gt))
                raise_flag(nc, dve, link, good[:].rearrange("p a n -> p (a n)"), bad, flag, bad_ready, bad_spread)


def output_projection(nc, sh, wo16, x1D, d, out, c):
    NT, DC, D = sh.NT, sh.DC, sh.D
    CT = 4
    NC = NT // CT
    with ExitStack() as ctx:
        s = Scope(nc, ctx, "op")
        at = s.sb("at", [P, NC, CT, D], F32)
        xt = s.sb("xt", [P, 2, CT, D], F32)
        atT = s.sb("atT", [P, 2, 2, D], F16)
        y = s.sb("y", [P, 2, CT, D], F32)
        psT = s.ps("psT", [P, 2, 512])
        psY = s.ps("psY", [P, 2, 512])

        at_in = [s.sem(f"at_in{n}") for n in range(NC)]
        x_in = [s.sem(f"x_in{k}") for k in range(2)]
        turned = s.sem("turned")
        hi_ready = s.sem("hi_ready")
        atT_ready = s.sem("atT_ready")
        projected = s.sem("projected")
        y_ready = s.sem("y_ready")
        y_out = [s.sem(f"y_out{k}") for k in range(2)]
        block = s.block()

        @block.gpsimd
        def _(pool):
            for k in range(2):
                pool.sem_inc(y_out[k], 16)

        @block.sync
        def _(sp):
            def load_x(n, k):
                sp.dma_start(xt[:, k], x1D[ds(n * (CT * P), CT * P), :].rearrange("(t p) d -> p t d", p=P)).then_inc(x_in[k], 16)

            for n in range(NC):
                sp.dma_start(at[:, n], d.att[n * CT * P:(n + 1) * CT * P, :].rearrange("(t p) d -> p t d", p=P)).then_inc(at_in[n], 16)
                if n < 2:
                    load_x(n, n)
            for n in range(NC):
                k = n % 2
                sp.wait_ge(y_ready, CT * n + 3 * CT)
                sp.dma_start(out[n * CT * P:(n + 1) * CT * P, :].rearrange("(t p) d -> p t d", p=P), y[:, k]).then_inc(y_out[k], 16)
                if n + 2 < NC:
                    load_x(n + 2, k)
            for k in range(2):
                sp.wait_ge(y_out[k], 16 * (NC // 2) + 16)

        @block.scalar
        def _(act):
            for t in range(NT):
                k = t % 2
                act.wait_ge(turned, t + 1)
                act.wait_ge(projected, t + 1)
                nc.scalar.activation(atT[:, k, 0, :], psT[:, k, :], ACT.Copy).then_inc(hi_ready, 1)

        @block.tensor
        def _(pe):
            pe.sem_inc(projected, 2)

            def turn(t):
                k = t % 2
                pe.wait_ge(at_in[t // CT], 16)
                pe.wait_ge(atT_ready, t + 1)
                for j in range(DC):
                    tr = nc.tensor.transpose(psT[:, k, j * P:(j + 1) * P], at[:, t // CT, t % CT, j * P:(j + 1) * P], c.ident[:])
                tr.then_inc(turned, 1)

            turn(0)
            for t in range(NT):
                k = t % 2
                if t + 1 < NT:
                    turn(t + 1)
                pe.wait_ge(atT_ready, t + 3)
                pe.wait_ge(y_ready, t + 2 * CT - 1)
                split_matmuls(nc, psY[:, k, :], [(atT[:, k, :, j * P:(j + 1) * P], wo16[:, j]) for j in range(DC)]).then_inc(projected, 1)

        @block.vector
        def _(dve):
            dve.sem_inc(atT_ready, 2)
            dve.sem_inc(y_ready, 2 * CT)

            def low(t):
                k = t % 2
                dve.wait_ge(hi_ready, t + 1)
                nc.vector.tensor_tensor(atT[:, k, 1, :], psT[:, k, :], atT[:, k, 0, :], ALU.subtract).then_inc(atT_ready, 1)

            low(0)
            for t in range(NT):
                n, m = t // CT, t % CT
                if t + 1 < NT:
                    low(t + 1)
                dve.wait_ge(projected, t + 3)
                if m == 0:
                    dve.wait_ge(x_in[n % 2], 16 * (n // 2) + 16)
                    dve.wait_ge(y_out[n % 2], 16 * (n // 2) + 16)
                nc.vector.scalar_tensor_tensor(y[:, n % 2, m, :], psY[:, t % 2, :], 1.0 / W_SCALE, xt[:, n % 2, m, :], ALU.mult, ALU.add).then_inc(y_ready, 1)


class Holder:
    pass


def two_graph_layers(nc, x, adj, w0, a_dst, wk, wq, wv, wo, out):
    sh = Shapes(x, w0)
    N, NT, H = sh.N, sh.NT, sh.H
    scale = float(sh.dh) ** -0.5
    mask_scale, diag_value = mask_constants(0.01 / scale)

    def dram(name, shape, dt):
        return nc.dram_tensor(name, shape, dt, kind="Internal").ap()

    maskD = dram("mask_tiles", (NT, P, N), F16)
    x1D = dram("x1", (N, sh.D), F32)
    d = Holder()
    d.qhi, d.qlo, d.khi, d.klo = (dram(n, (sh.D, N), F16) for n in ("q_high", "q_low", "k_high", "k_low"))
    d.v = dram("v_parts", (H, P, NT * sh.VC), F16)
    d.shift = dram("shift", (H, N), F16)
    d.att = dram("att", (N, sh.D), F32)
    d.t_hi, d.t_lo = dram("t_high", (H, N), F16), dram("t_low", (H, N), F16)
    plainD = dram("plain_mask_tiles", (NT, P, N), F16)

    with ExitStack() as ctx:
        s = Scope(nc, ctx, "all")
        c = Holder()
        c.ident = s.sb("ident", [P, P], F32)
        c.ident_bf = s.sb("ident_bf", [P, P], BF16)
        c.mask_ident = s.sb("mask_ident", [P, P], F16)
        c.diag_mask = s.sb("diag_mask", [P, P], F16)
        mv1 = s.sb("mv1", [P, NT, 2], F32)
        make_constants(nc, c, mask_scale, diag_value)
        flag0 = s.sb("flag0", [1, 1], I32)
        flag1 = s.sb("flag1", [1, 1], I32)

        with ExitStack() as ctx0:
            s0 = Scope(nc, ctx0, "l0")
            emx = s0.sb("emx", [P, NT, 2, 2 * sh.GC], F16)
            with ExitStack() as ctx1:
                s1 = Scope(nc, ctx1, "l0v")
                xm = s1.sb("xm", [P, NT, sh.D], F32)
                t_all = s1.sb("t_all", [P, NT, H], F32)
                gat_values(nc, sh, x, w0, a_dst, xm, t_all, emx, c)
            gat_attention(nc, sh, x, adj, emx, mv1, maskD, x1D, flag0, c)
        with nc.If(nc.values_load(flag0[0:1, 0:1], min_val=0, max_val=1) > 0):
            with ExitStack() as ctx1:
                s1 = Scope(nc, ctx1, "l0r")
                xm = s1.sb("xm", [P, NT, sh.D], F32)
                t_all = s1.sb("t_all", [P, NT, H], F32)
                gat_values(nc, sh, x, w0, a_dst, xm, t_all, None, c)
                scores_for_attention(nc, sh, xm, t_all, d, c)
            plain_masks(nc, sh, adj, plainD, c)
            row_maxima(nc, sh, adj, d, c, "mx0", False)
            attention(nc, sh, plainD, d, c, scale, "at0", True, None)
            add_residual(nc, sh, x, d, mv1, x1D)
        wo16 = s.sb("wo16", [P, sh.DC, 2, sh.D], F16)
        qkv(nc, sh, x1D, wq, wk, wv, wo, wo16, mv1, d, c)
        attention(nc, sh, maskD, d, c, scale, "at", False, flag1)
        with nc.If(nc.values_load(flag1[0:1, 0:1], min_val=0, max_val=1) > 0):
            row_maxima(nc, sh, adj, d, c, "mx", True)
            attention(nc, sh, maskD, d, c, scale, "at2", True, None)
        output_projection(nc, sh, wo16, x1D, d, out, c)


_INS = ["x", "adj", "L0_gnn_W", "L0_gnn_a_dst", "L1_gnn_Wks", "L1_gnn_Wqs", "L1_gnn_Wvs", "L1_gnn_Wo"]


def kernel(**inputs):
    import numpy as _np
    import concourse.bacc as _bacc
    from concourse import mybir as _mybir
    from concourse.bass_utils import run_bass_kernel_spmd as _run

    nc = _bacc.Bacc("TRN2", target_bir_lowering=False, num_devices=1)
    arrays, args = {}, []
    for name in _INS:
        a = _np.ascontiguousarray(inputs[name])
        arrays[f"in_{name}"] = a
        args.append(nc.dram_tensor(f"in_{name}", a.shape, _mybir.dt.from_np(a.dtype), kind="ExternalInput").ap())
    out = nc.dram_tensor("out_x", inputs["x"].shape, _mybir.dt.float32, kind="ExternalOutput").ap()
    two_graph_layers(nc, *args, out)
    r = _run(nc, [arrays], core_ids=[0])
    return r.results[0]["out_x"]
```
